# Optimizing a Trainium2 kernel written in Bass

```python
import numpy as np
import jax
import jax.numpy as jnp

def _softmax(x, axis=-1):
    return jax.nn.softmax(x, axis=axis)

def _gelu(x):
    return jax.nn.gelu(x, approximate=True)

def _silu(x):
    return jax.nn.silu(x)

def _sigmoid(x):
    return jax.nn.sigmoid(x)

def _layernorm(x, axis=-1, eps=1e-05):
    m = jnp.mean(x, axis=axis, keepdims=True)
    v = jnp.var(x, axis=axis, keepdims=True)
    return (x - m) / jnp.sqrt(v + eps)

def _scatter_add(tgt, idx, src, axis=0):
    return tgt.at[idx].add(src)

def _segment_sum(src, seg, n):
    return jax.ops.segment_sum(src, seg, n)
kernel_name = 'mk_flamingo_gated_d1_seqx_r2_0bf9e9'

def setup_inputs(seed: int=0):
    np.random.seed(seed)
    _w = jnp.asarray

    def _rec_inputs():
        import jax
        import jax.numpy as jnp
        _rk = jax.random.key(seed)
        x = 7.22e-05 + 1 * jax.random.normal(jax.random.fold_in(_rk, 1), (16, 256, 1024), jnp.float32)
        _lenS = 256 - jax.random.randint(jax.random.fold_in(_rk, 7), (16,), 0, max(1, 256 // 4) + 1, jnp.int32)
        _lenS2 = 256 - jax.random.randint(jax.random.fold_in(_rk, 8), (16,), 0, max(1, 256 // 4) + 1, jnp.int32)
        _ctx_512P = jax.random.normal(jax.random.fold_in(_rk, 11), (16, 16, 256), jnp.float32)
        _ctx_512c = jax.random.dirichlet(jax.random.fold_in(_rk, 511), 0.3 * jnp.ones((16,), jnp.float32), (16, 256))
        _ctx_512t = jnp.einsum('bsk,bkd->bsd', _ctx_512c, _ctx_512P)
        _ctx_512t = _ctx_512t * jax.lax.rsqrt(jnp.mean(jnp.square(_ctx_512t)) + 1e-12) * 0.953939
        ctx_512 = -0.000514642 + 1.00011 * (_ctx_512t + 0.3 * jax.random.normal(jax.random.fold_in(_rk, 611), (16, 256, 256), jnp.float32))
        _g = jax.random.normal(jax.random.fold_in(_rk, 9001), (2, 1), jnp.float32)
        _g = jnp.sign(_g) * jnp.maximum(jnp.abs(_g), 1.0) + (_g == 0) * 1.0
        g_xattn = _g[0]
        g_ffn = _g[1]
        return (x, ctx_512, g_xattn, g_ffn)
    x, ctx_512, g_xattn, g_ffn = _rec_inputs()

    def _L0_xattn_setup():
        import jax, jax.numpy as jnp
        import numpy as np
        B, S, E = (2, 1024, 1024)
        QH, KVH = (32, 8)
        D = E // QH
        G = QH // KVH
        DROPOUT = 1.0
        key = jax.random.key(seed)
        k1, k2, k3 = jax.random.split(key, 3)
        q = jax.random.normal(k1, (B, S, E), dtype=jnp.float32)
        k = jax.random.normal(k2, (B, S, E // G), dtype=jnp.float32)
        v = jax.random.normal(k3, (B, S, E // G), dtype=jnp.float32)
        return {'q': q, 'k': k, 'v': v}
    _L0_xattn_all = _L0_xattn_setup()
    _L0_xattn_in = {k: v for k, v in _L0_xattn_all.items() if k in ()}
    del _L0_xattn_all

    def _L0_ffn_setup():
        import jax, jax.numpy as jnp
        import numpy as np
        B, S, H = (2, 512, 1024)
        I = 512
        E = 32
        Z = 32
        K = 8
        SCALE = 1.5
        CAP = 512
        EPS = 1e-20

        def _moe_forward(x, w_cls, bias, w_gate_up, w_down):
            T = x.shape[0] * x.shape[1]
            xf = x.reshape(T, H)
            logits = xf.astype(jnp.float32) @ w_cls.T
            scores = jax.nn.softmax(logits, axis=-1)
            _, topk_idx = jax.lax.top_k(scores + bias[None, :], K)
            w = jnp.take_along_axis(scores, topk_idx, axis=-1)
            w = w / (w.sum(-1, keepdims=True) + EPS) * SCALE
            routed = topk_idx < E
            w_r = jnp.where(routed, w, 0.0)
            w_z = jnp.where(routed, 0.0, w)
            N = T * K
            flat_ids = jnp.where(routed, topk_idx, E).reshape(-1)
            x_exp = jnp.repeat(xf, K, axis=0)
            order = jnp.argsort(flat_ids)
            ids_s = flat_ids[order]
            counts = jax.ops.segment_sum(jnp.ones(N, jnp.int32), flat_ids, num_segments=E + 1)
            starts = jnp.cumsum(counts) - counts
            pos = jnp.arange(N) - starts[ids_s]
            buf = jnp.zeros((E, CAP, H), xf.dtype).at[ids_s, pos].set(x_exp[order], mode='drop')
            gu = jnp.einsum('ech,ehf->ecf', buf, w_gate_up)
            g, u = jnp.split(gu, 2, axis=-1)
            act = jax.nn.silu(g) * u
            y = jnp.einsum('eci,eih->ech', act, w_down)
            valid = (ids_s < E) & (pos < CAP)
            y_tok = jnp.where(valid[:, None], y[jnp.clip(ids_s, 0, E - 1), jnp.clip(pos, 0, CAP - 1)], 0.0)
            y_exp = jnp.zeros((N, H), xf.dtype).at[order].set(y_tok).reshape(T, K, H)
            routed_out = jnp.einsum('tk,tkh->th', w_r, y_exp)
            out = routed_out * (1.0 + w_z.sum(-1, keepdims=True))
            return out.reshape(x.shape)
        key = jax.random.key(seed)
        ks = jax.random.split(key, 5)
        x = jax.random.normal(ks[0], (B, S, H), jnp.float32)
        w_cls = jax.random.normal(ks[1], (E + Z, H), jnp.float32) / np.float32(np.sqrt(H))
        bias = jax.random.normal(ks[2], (E + Z,), jnp.float32) * 0.02
        w_gate_up = jax.random.normal(ks[3], (E, H, 2 * I), jnp.float32) * 0.02
        w_down = jax.random.normal(ks[4], (E, I, H), jnp.float32) * 0.02
        return {'x': x, 'w_cls': w_cls, 'bias': bias, 'w_gate_up': w_gate_up, 'w_down': w_down}
    _L0_ffn_all = _L0_ffn_setup()
    _L0_ffn_in = {k: v for k, v in _L0_ffn_all.items() if k in ('w_cls', 'bias', 'w_gate_up', 'w_down')}
    del _L0_ffn_all
    return {'x': x, 'ctx_512': ctx_512, 'g_xattn': g_xattn, 'g_ffn': g_ffn, 'L0_ffn_w_cls': _L0_ffn_in['w_cls'], 'L0_ffn_bias': _L0_ffn_in['bias'], 'L0_ffn_w_gate_up': _L0_ffn_in['w_gate_up'], 'L0_ffn_w_down': _L0_ffn_in['w_down']}

def reference(x, ctx_512, g_xattn, g_ffn, L0_ffn_w_cls, L0_ffn_bias, L0_ffn_w_gate_up, L0_ffn_w_down):
    import jax
    import jax.numpy as jnp

    def _L0_xattn_ref(q, k, v):
        import jax, jax.numpy as jnp
        import numpy as np
        B, S, E = (2, 1024, 1024)
        QH, KVH = (32, 8)
        D = E // QH
        G = QH // KVH
        DROPOUT = 1.0
        b, s, _ = q.shape
        qh = q.reshape(b, s, KVH, G, D).transpose(0, 2, 3, 1, 4)
        kh = k.reshape(b, s, KVH, D).transpose(0, 2, 1, 3)
        vh = v.reshape(b, s, KVH, D).transpose(0, 2, 1, 3)
        scale = 1.0 / jnp.sqrt(jnp.float32(D))
        scores = jnp.einsum('bkgsd,bktd->bkgst', qh, kh) * scale
        attn = jax.nn.softmax(scores, axis=-1) / DROPOUT
        out = jnp.einsum('bkgst,bktd->bkgsd', attn, vh)
        return out.transpose(0, 3, 1, 2, 4).reshape(b, s, E)

    def _L0_ffn_ref(x, w_cls, bias, w_gate_up, w_down):
        import jax, jax.numpy as jnp
        import numpy as np
        B, S, H = (2, 512, 1024)
        I = 512
        E = 32
        Z = 32
        K = 8
        SCALE = 1.5
        CAP = 512
        EPS = 1e-20

        def _moe_forward(x, w_cls, bias, w_gate_up, w_down):
            T = x.shape[0] * x.shape[1]
            xf = x.reshape(T, H)
            logits = xf.astype(jnp.float32) @ w_cls.T
            scores = jax.nn.softmax(logits, axis=-1)
            _, topk_idx = jax.lax.top_k(scores + bias[None, :], K)
            w = jnp.take_along_axis(scores, topk_idx, axis=-1)
            w = w / (w.sum(-1, keepdims=True) + EPS) * SCALE
            routed = topk_idx < E
            w_r = jnp.where(routed, w, 0.0)
            w_z = jnp.where(routed, 0.0, w)
            N = T * K
            flat_ids = jnp.where(routed, topk_idx, E).reshape(-1)
            x_exp = jnp.repeat(xf, K, axis=0)
            order = jnp.argsort(flat_ids)
            ids_s = flat_ids[order]
            counts = jax.ops.segment_sum(jnp.ones(N, jnp.int32), flat_ids, num_segments=E + 1)
            starts = jnp.cumsum(counts) - counts
            pos = jnp.arange(N) - starts[ids_s]
            buf = jnp.zeros((E, CAP, H), xf.dtype).at[ids_s, pos].set(x_exp[order], mode='drop')
            gu = jnp.einsum('ech,ehf->ecf', buf, w_gate_up)
            g, u = jnp.split(gu, 2, axis=-1)
            act = jax.nn.silu(g) * u
            y = jnp.einsum('eci,eih->ech', act, w_down)
            valid = (ids_s < E) & (pos < CAP)
            y_tok = jnp.where(valid[:, None], y[jnp.clip(ids_s, 0, E - 1), jnp.clip(pos, 0, CAP - 1)], 0.0)
            y_exp = jnp.zeros((N, H), xf.dtype).at[order].set(y_tok).reshape(T, K, H)
            routed_out = jnp.einsum('tk,tkh->th', w_r, y_exp)
            out = routed_out * (1.0 + w_z.sum(-1, keepdims=True))
            return out.reshape(x.shape)
        return _moe_forward(x, w_cls, bias, w_gate_up, w_down)
    x = x + jnp.tanh(g_xattn[0]) * _L0_xattn_ref(_layernorm(x, axis=-1), ctx_512, ctx_512)
    x = x + jnp.tanh(g_ffn[0]) * _L0_ffn_ref(_layernorm(x, axis=-1), L0_ffn_w_cls, L0_ffn_bias, L0_ffn_w_gate_up, L0_ffn_w_down)
    return x

_drawn_inputs = setup_inputs


def setup_inputs(seed=0):
    import zlib

    import numpy as np

    out = dict(_drawn_inputs(seed))
    spreads = {}
    factors = {}
    for name, (base, spread) in spreads.items():
        noise = np.random.default_rng([zlib.crc32(name.encode()), seed]).standard_normal(out[name].shape)
        drawn = base * np.exp(spread * noise) if base else spread * noise
        out[name] = jnp.asarray(drawn.astype(out[name].dtype))
    for name, factor in factors.items():
        out[name] = (out[name] * factor).astype(out[name].dtype)
    return out
```

```python
from contextlib import ExitStack

import concourse.bass as bass
from concourse import mybir

F32 = mybir.dt.float32
F16 = mybir.dt.float16
I32 = mybir.dt.int32
U32 = mybir.dt.uint32
ALU = mybir.AluOpType
ACT = mybir.ActivationFunctionType
AXX = mybir.AxisListType.X

P = 128
D = 32
G = 4
KV = 8
NH = G * KV
S = 256
T2 = S // P
H = NH * D
KB = H // P
NROUTED = 32
NALL = 64
TOPK = 8
CAP = 512
CT = CAP // P
FF = 512
FB = FF // P
ROUTE_SCALE = 1.5
LN_EPS = 1e-5
ROUTE_EPS = 1e-20

XS_SCALE = 64.0
C_SCALE = 16.0
W_SCALE = 256.0
A_SCALE = 32.0
M_SCALE = 32768.0
P_LOG = 12
NO_SLOT = float(1 << 20)

TR_P, TR_R = 12, 6
CHUNKS = FB + 2
WRING = 3


class Tally:

    def __init__(self, engine, sem, base=0):
        self.engine, self.sem, self.base, self.n = engine, sem, base, 0

    def add(self, instruction):
        instruction.then_inc(self.sem, 1)
        self.n += 1
        return self.base + self.n

    def wait(self, value=None):
        self.engine.wait_ge(self.sem, self.base + self.n if value is None else value)

    def close(self, steps):
        assert self.n == steps, (self.n, steps)


def gated_block_kernel(nc, x, ctx_512, g_xattn, g_ffn, w_cls, bias, w_gate_up, w_down, out, nb=16, ne=NROUTED):
    ntok = nb * S
    x_v = x.rearrange("b (t p) h -> b p t h", p=P)
    c_v = ctx_512.rearrange("b (t p) h -> b p t h", p=P)
    o_v = out.rearrange("b (t p) h -> b p t h", p=P)
    o_rows = out.rearrange("b s h -> (b s) h")
    gu_v = w_gate_up.rearrange("e (k p) (h f) -> e p k h f", p=P, h=2)
    dn_v = w_down.rearrange("e (k p) h -> e p k h", p=P)
    pairs = nc.dram_tensor("pairs", [ntok, 2 * H], F16).ap()
    lists = nc.dram_tensor("lists", [NROUTED * CAP, 2], I32).ap()
    pairs_v = pairs.rearrange("(b t p) h -> b p t h", p=P, t=T2)
    lists_v = lists.rearrange("(e c p) w -> e p c w", p=P, c=CT)
    lists_all = lists.rearrange("(p a) w -> p (a w)", p=P)

    with ExitStack() as whole:
        stack = [whole]

        def sb(name, shape, dt=F32):
            return stack[-1].enter_context(nc.sbuf_tensor(name, shape, dt))

        def sem(name):
            return whole.enter_context(nc.semaphore(name))

        psum = whole.enter_context(nc.psum_tensor("psum", [P, 8, 512], F32))

        ident = sb("ident", [P, P], F16)
        spare = sb("spare", [P, 4])
        filled = sb("filled", [1, NROUTED], I32)
        wraw = sb("wraw", [P, WRING, 2048])
        wpair = sb("wpair", [P, WRING, 2, 2048], F16)

        first = ExitStack()
        stack.append(first)
        x1 = sb("x1", [P, T2, H])
        xr = sb("xr", [P, T2, H])
        xn = sb("xn", [P, T2, H])
        cx = sb("cx", [P, T2, KV, D])
        qd = sb("qd", [P, T2, NH, 3, D], F16)
        kd = sb("kd", [P, 2, T2, KV, 98], F16)
        qs = sb("qs", [98, 2, NH, S], F16)
        ks = sb("ks", [98, 2, KV, S], F16)
        mx = sb("mx", [P, T2, NH])
        mpair = sb("mpair", [P, 2, T2, 2, NH // 2], F16)
        mrow = sb("mrow", [32, 2, S], F16)
        prob = sb("prob", [P, 2, G * S])
        phi = sb("phi", [P, 4, G * S], F16)
        plo = sb("plo", [P, 4, G * S], F16)
        at = sb("at", [P, T2, NH, D])
        x2 = sb("x2", [P, T2, H])
        xs = sb("xs", [P, T2, 2, H], F16)
        xt = sb("xt", [P, 2, T2, KB, P], F16)
        wc = sb("wc", [P, KB, 2, NALL], F16)
        stats = sb("stats", [P, 2, T2, 2, 6])
        mv = sb("mv", [P, 2, T2, 2])
        veps = sb("veps", [P, 2, T2])
        rstd = sb("rstd", [P, 2, T2])
        nmr = sb("nmr", [P, 2, T2])
        half = sb("half", [P, T2])
        pbias = sb("pbias", [P, 1])
        recip = sb("recip", [P, T2, G])
        gates = sb("gates", [P, 2])
        tgate = sb("tgate", [P, 2])
        tg_at = sb("tg_at", [P, 1])
        tg_ff = sb("tg_ff", [P, 1])
        bias_b = sb("bias_b", [P, NALL])
        tri = sb("tri", [P, P], F16)
        ones = sb("ones", [P, P], F16)
        iota_e = sb("iota_e", [P, NROUTED])
        slot0 = sb("slot0", [P, NROUTED])
        token = sb("token", [P, T2, TOPK])
        lg = sb("lg", [P, T2, NALL])
        lmax = sb("lmax", [P, T2])
        lneg = sb("lneg", [P, T2])
        lexp = sb("lexp", [P, T2, NALL])
        lsum = sb("lsum", [P, T2])
        lrec = sb("lrec", [P, T2])
        score = sb("score", [P, T2, NALL])
        biased = sb("biased", [P, T2, NALL])
        top = sb("top", [P, T2, TOPK])
        topi = sb("topi", [P, T2, TOPK], U32)
        topf = sb("topf", [P, T2, TOPK])
        left = sb("left", [P, T2, NALL])
        mask = sb("mask", [P, T2, NALL], F16)
        wsel = sb("wsel", [P, T2, NALL])
        wsum = sb("wsum", [P, T2, 1])
        wzero = sb("wzero", [P, T2, 1])
        wrec = sb("wrec", [P, T2, 1])
        wfac = sb("wfac", [P, T2, 1])
        coef = sb("coef", [P, T2, NROUTED])
        pos = sb("pos", [P, T2, NROUTED])
        place = sb("place", [P, T2, NROUTED])
        carry = sb("carry", [P, NROUTED])
        hot = sb("hot", [P, T2, TOPK, NROUTED])
        pick = sb("pick", [P, 2, T2, TOPK, NROUTED])
        picked = sb("picked", [P, 2, T2 * TOPK])
        dest = sb("dest", [P, T2 * TOPK], I32)
        entry = sb("entry", [P, T2 * TOPK, 2], I32)
        wcraw = at[0:NALL, 0].rearrange("p h d -> p (h d)")
        wcpair = phi[0:NALL, 0:2, :]
        empty = sb("empty", [P, NROUTED * CT, 2], I32)
        stack.pop()
        first.close()

        xg = sb("xg", [P, CT, 2, H], F16)
        xgt = sb("xgt", [P, 2, 2, KB, CAP], F16)
        slots = sb("slots", [P, 2, CT, 2], I32)
        sg = sb("sg", [P, 2, CAP])
        a32 = sb("a32", [P, 2, CAP])
        apair = sb("apair", [P, 2, FB, CAP], F16)
        ys = sb("ys", [P, CT, H])

        ps_s = psum[:, 0:2, :]
        ps_t = psum[:, 2:6, :].rearrange("p (r b) n -> p r (b n)", r=2)
        ps_v = psum[:, 6, 0:T2 * G * 33].rearrange("p (t g d) -> p t g d", t=T2, g=G)
        ps_x = psum[:, 7, :]
        ps_x16 = psum[:, 7, :].bitcast(F16)
        ps_gu = psum[:, 0:4, :].rearrange("p (r h) n -> p r h n", r=2)
        ps_y = psum[:, 4:6, :]
        ps_g16 = [psum[:, 6, :].bitcast(F16), psum[:, 7, :].bitcast(F16)]

        small_in = sem("small_in")
        x1_in, cx_in, xr_in = sem("x1_in"), sem("cx_in"), sem("xr_in")
        mrow_in = [sem("mrow_in0"), sem("mrow_in1")]
        x2_out, pairs_out = sem("x2_out"), sem("pairs_out")
        lists_set, lists_out = sem("lists_set"), sem("lists_out")
        w_in = [sem(f"w_in{i}") for i in range(WRING)]
        slots_in = [sem("slots_in0"), sem("slots_in1")]
        gathered = sem("gathered")
        added = sem("added")
        consts = sem("consts")
        dve_order = sem("dve_order")
        pool_order = sem("pool_order")
        setup_dve = sem("setup_dve")
        setup_act = sem("setup_act")
        wc_t = sem("wc_t")
        var_ready = sem("var_ready")
        rstd_ready = sem("rstd_ready")
        nmr_ready = sem("nmr_ready")
        qhi_ready = sem("qhi_ready")
        qd_ready = sem("qd_ready")
        khi_ready = sem("khi_ready")
        kd_ready = sem("kd_ready")
        x_full, x_free = sem("x_full"), sem("x_free")
        s_full, s_free = sem("s_full"), sem("s_free")
        stack_ready = sem("stack_ready")
        mpair_ready = sem("mpair_ready")
        t_full, t_free = sem("t_full"), sem("t_free")
        phi_ready = sem("phi_ready")
        plo_dve, plo_pool = sem("plo_dve"), sem("plo_pool")
        v_full, v_free = sem("v_full"), sem("v_free")
        x2_ready = sem("x2_ready")
        xhi_ready = sem("xhi_ready")
        xs_ready = sem("xs_ready")
        lneg_ready, lexp_ready = sem("lneg_ready"), sem("lexp_ready")
        mask_ready = sem("mask_ready")
        entry_ready = sem("entry_ready")
        stage1 = sem("stage1")
        wpair_hi, wpair_lo = sem("wpair_hi"), sem("wpair_lo")
        gt_full, gt_free = sem("gt_full"), sem("gt_free")
        gu_full = sem("gu_full")
        sg_ready, a32_ready = sem("sg_ready"), sem("a32_ready")
        ahi_ready, alo_ready = sem("ahi_ready"), sem("alo_ready")
        y_full, y_free = sem("y_full"), sem("y_free")

        def fills_p(b):
            return 0 if isinstance(b, int) and b == 0 else (TR_P + TR_R) * (b - 1) + TR_P

        def fills_r(b):
            last = isinstance(b, int) and b == nb - 1
            return (TR_P + TR_R) * b + (TR_P if last else 2 * TR_P)

        def fill_q(b, kv):
            return fills_p(b) + 2 + kv + (1 if kv >= 6 else 0)

        def fill_m(b, hf):
            return fills_p(b) + (11 if hf else 8)

        def loops(eng, step):
            step(0, 0, False)
            with eng.Fori(0, (nb - 2) // 2) as i:
                step(2 * i + 1, 1, False)
                step(2 * i + 2, 0, False)
            step(nb - 1, 1, True)

        def loops2(eng, step):
            step(0, 0, False)
            with eng.Fori(0, (ne - 2) // 2) as i:
                step(2 * i + 1, 1, False)
                step(2 * i + 2, 0, False)
            step(ne - 1, 1, True)

        def is_first(b):
            return isinstance(b, int) and b == 0


        block = whole.enter_context(nc.Block())

        @block.sync
        def _(sp):
            sp.dma_start(gates[:, 0:1], g_xattn.rearrange("(a b) -> a b", a=1).to_broadcast([P, 1])).then_inc(small_in, 16)
            sp.dma_start(gates[:, 1:2], g_ffn.rearrange("(a b) -> a b", a=1).to_broadcast([P, 1])).then_inc(small_in, 16)
            sp.dma_start(bias_b[:], bias.rearrange("(a b) -> a b", a=1).to_broadcast([P, NALL])).then_inc(small_in, 16)
            sp.dma_start(wcraw, w_cls).then_inc(small_in, 16)
            sp.dma_start(x1[:], x_v[0]).then_inc(x1_in, 16)
            sp.dma_start(cx[:], c_v[0].rearrange("p t (k d) -> p t k d", d=D)).then_inc(cx_in, 16)
            sp.wait_ge(consts, 1)
            sp.dma_start(lists_all, empty[:].rearrange("p a w -> p (a w)")).then_inc(lists_set, 16)

            def load_next(b):
                sp.wait_ge(qd_ready, b)
                sp.wait_ge(kd_ready, b)
                sp.dma_start(x1[:], x_v[b]).then_inc(x1_in, 16)
                sp.dma_start(cx[:], c_v[b].rearrange("p t (k d) -> p t k d", d=D)).then_inc(cx_in, 16)

            def maxima(b, par):
                for hf in range(2):
                    sp.wait_ge(x_free, fill_m(b, hf) + 1)
                    hs = hf * NH // 2
                    for part in range(2):
                        sp.dma_start(qs[96 + part:97 + part, par, hs:hs + NH // 2, :],
                                     mrow[16 * part:16 * part + 16, hf, :]).then_inc(mrow_in[hf], 16)

            def store(b):
                sp.wait_ge(x2_ready, b + 1)
                sp.dma_start(o_v[b], x2[:]).then_inc(x2_out, 16)
                sp.wait_ge(xs_ready, b + 1)
                sp.dma_start(pairs_v[b], xs[:].rearrange("p t a h -> p t (a h)")).then_inc(pairs_out, 16)

            def step(b, par, last):
                if not is_first(b):
                    store(b - 1)
                    sp.wait_ge(x2_ready, b)
                sp.dma_start(xr[:], x_v[b]).then_inc(xr_in, 16)
                if not last:
                    if not (isinstance(b, int) and b == nb - 2):
                        pass
                    maxima(b + 1, 1 - par)

            load_next_limit = nb

            maxima(0, 0)

            def full_step(b, par, last):
                if not last and not (isinstance(b, int) and b >= load_next_limit - 1):
                    load_next(b + 1)
                step(b, par, last)

            loops(sp, full_step)
            store(nb - 1)

            def weights(e, i):
                r = i % WRING
                n = CHUNKS * e + i
                if not (isinstance(n, int) and n < WRING):
                    sp.wait_ge(wpair_lo, n - WRING + 1)
                if i < FB:
                    for h in range(2):
                        sp.dma_start(wraw[:, r, :].rearrange("p (k h f) -> p k h f", k=KB, h=2)[:, :, h, :],
                                     gu_v[e][:, :, h, i * P:(i + 1) * P]).then_inc(w_in[r], 16)
                else:
                    for h in range(2):
                        sp.dma_start(wraw[:, r, h * 1024:(h + 1) * 1024].rearrange("p (k f) -> p k f", k=FB // 2),
                                     dn_v[e][:, 2 * h:2 * h + 2, (i - FB) * 512:(i - FB + 1) * 512]).then_inc(w_in[r], 16)

            def get_slots(e, par):
                if not (isinstance(e, int) and e < 2):
                    sp.wait_ge(added, 16 * CT * (e - 1))
                sp.dma_start(slots[:, par], lists_v[e]).then_inc(slots_in[par], 16)

            for i in range(WRING):
                weights(0, i)
            sp.wait_ge(lists_out, 16 * T2 * TOPK * nb)
            sp.wait_ge(stage1, 4)
            sp.wait_ge(x2_out, 16 * nb)
            sp.wait_ge(pairs_out, 16 * nb)
            get_slots(0, 0)

            def step2(e, par, last):
                if not last:
                    get_slots(e + 1, 1 - par)
                for i in range(WRING, CHUNKS):
                    weights(e, i)
                if not last:
                    for i in range(WRING):
                        weights(e + 1, i)

            loops2(sp, step2)
            sp.wait_ge(added, 16 * CT * ne)

        @block.gpsimd
        def _(pool):
            def const(ins):
                ins.then_inc(pool_order, 1)
                pool_n[0] += 1
                pool.wait_ge(pool_order, pool_n[0])
            pool_n = [0]
            const(pool.iota(empty[:], pattern=[[0, NROUTED * CT], [0, 2]], base=int(NO_SLOT), channel_multiplier=0))
            pool.memset(ident[:], 0.0).then_inc(consts, 1)
            pool.wait_ge(consts, 1)
            const(pool.affine_select(out=ident[:], in_=ident[:], compare_op=ALU.not_equal, fill=1.0, base=0,
                                     pattern=[[-1, P]], channel_multiplier=1))
            const(pool.memset(ones[:], 1.0))
            const(pool.affine_select(out=tri[:], in_=ones[:], compare_op=ALU.is_gt, fill=0.0, base=0,
                                     pattern=[[1, P]], channel_multiplier=-1))
            const(pool.iota(iota_e[:], pattern=[[1, NROUTED]], base=0, channel_multiplier=0,
                            allow_small_or_imprecise_dtypes=True))
            const(pool.iota(slot0[:], pattern=[[CAP, NROUTED]], base=-int(NO_SLOT), channel_multiplier=0,
                            allow_small_or_imprecise_dtypes=True))
            const(pool.iota(token[:], pattern=[[P, T2], [0, TOPK]], base=0, channel_multiplier=1,
                            allow_small_or_imprecise_dtypes=True))
            const(pool.memset(half[:], -0.5))
            const(pool.memset(spare[:, 3:4], 0.0))
            const(pool.memset(pbias[:], P_LOG * 0.6931471805599453))
            const(pool.memset(carry[:], 0.0))
            const(pool.memset(kd[:], 1.0))
            const(pool.memset(ks[96:98, :, :, :], M_SCALE))
            pool.memset(half[:], -0.5).then_inc(consts, 1)
            pool.wait_ge(consts, 2)
            n0 = pool_n[0]

            def carry_wait(n):
                pool.wait_ge(pool_order, n0 + n)
                pool.tensor_tensor(spare[:, 2:3], spare[:, 3:4], spare[:, 3:4], ALU.mult).then_inc(pool_order, 1)

            def power(which, n):
                pool.wait_ge(var_ready, n)
                pool.tensor_tensor(rstd[:, which], veps[:, which], half[:], ALU.pow).then_inc(rstd_ready, 1)

            def norm1(b):
                power(0, 1 if is_first(b) else 2 * b)

            def norm2(b, last=False):
                power(1, 2 * b + 3 - (1 if last else 0))

            def low_probs(b, kv):
                u = 16 * b + 2 * kv + 1
                pool.wait_ge(phi_ready, u + 1)
                if not (isinstance(u, int) and u < 4):
                    pool.wait_ge(v_full, 8 * b + kv - 1)
                r = (2 * kv + 1) % 4
                pool.tensor_tensor(plo[:, r], prob[:, 1], phi[:, r], ALU.subtract).then_inc(plo_pool, 1)

            def scatter(b, n0, n1):
                if n0 == 0:
                    pool.wait_ge(entry_ready, b + 1)
                    carry_wait(b)
                for n in range(n0, n1):
                    pool.indirect_dma_start(
                        out=lists, out_offset=bass.IndirectOffsetOnAxis(ap=dest[:, n:n + 1].bitcast(U32), axis=0),
                        in_=entry[:, n, :], in_offset=None, bounds_check=NROUTED * CAP - 1,
                        oob_is_err=False).then_inc(lists_out, 16)

            def step(b, par, last):
                if not is_first(b):
                    norm2(b - 1)
                if not last:
                    norm1(b + 1)
                for kv in range(KV):
                    low_probs(b, kv)
                    if not is_first(b) and kv >= 4:
                        scatter(b - 1, (kv - 4) * 4, (kv - 3) * 4)

            norm1(0)
            pool.wait_ge(lists_set, 16)
            loops(pool, step)
            norm2(nb - 1, True)
            scatter(nb - 1, 0, T2 * TOPK)
            pool.wait_ge(lists_out, 16 * T2 * TOPK * nb)
            pool.memset(slots[:], 0).then_inc(stage1, 1)
            pool.wait_ge(stage1, 4)
            pool.wait_ge(pairs_out, 16 * nb)
            pool.wait_ge(x2_out, 16 * nb)
            pool.memset(xg[:], 0.0).then_inc(pool_order, 1)
            n0 += nb + 1
            pool.wait_ge(pool_order, n0)

            def gather(e, par):
                pool.wait_ge(slots_in[par], 8 * e + 16 if par == 0 else 8 * (e + 1))
                if not is_first(e):
                    pool.wait_ge(gt_full, 8 * e)
                carry_wait(0 if is_first(e) else (CT + 1) * (e - 1) + 1)
                for c in range(CT):
                    pool.indirect_dma_start(
                        out=xg[:, c].rearrange("p a h -> p (a h)"), out_offset=None, in_=pairs,
                        in_offset=bass.IndirectOffsetOnAxis(ap=slots[:, par, c, 0:1].bitcast(U32), axis=0),
                        bounds_check=ntok - 1, oob_is_err=False).then_inc(gathered, 16)

            def add(e, par, last):
                if not is_first(e):
                    pool.wait_ge(added, 16 * CT * e)
                for c in range(CT):
                    pool.wait_ge(y_free, 8 * e + 5 + c)
                    carry_wait((CT + 1) * e + c + (2 if not last else 1))
                    pool.indirect_dma_start(
                        out=o_rows, out_offset=bass.IndirectOffsetOnAxis(ap=slots[:, par, c, 0:1].bitcast(U32), axis=0),
                        in_=ys[:, c, :], in_offset=None, bounds_check=ntok - 1, oob_is_err=False,
                        compute_op=ALU.add).then_inc(added, 16)

            def step2(e, par, last):
                if not last:
                    gather(e + 1, 1 - par)
                add(e, par, last)

            gather(0, 0)
            loops2(pool, step2)
            pool.wait_ge(added, 16 * CT * ne)

        @block.scalar
        def _(act):
            act.wait_ge(small_in, 64)
            act.activation(tgate[:], gates[:], ACT.Tanh).then_inc(setup_act, 1)
            act.activation(wcpair[:, 0, :], wcraw, ACT.Copy, scale=W_SCALE).then_inc(setup_act, 1)
            act.wait_ge(consts, 2)

            def hi_q(b):
                act.wait_ge(nmr_ready, 1 if is_first(b) else 2 * b)
                if not is_first(b):
                    act.wait_ge(x_full, fill_q(b - 1, KV - 1) + 1)
                for t in range(T2):
                    for c in range(2):
                        act.activation(qd[:, t, :, c, :], x1[:, t].rearrange("p (h d) -> p h d", d=D), ACT.Identity,
                                       scale=rstd[:, 0, t:t + 1], bias=nmr[:, 0, t:t + 1]).then_inc(qhi_ready, 1)

            def hi_k(b, par):
                act.wait_ge(cx_in, 16 * (b + 1))
                if not (isinstance(b, int) and b < 2):
                    act.wait_ge(v_full, 8 * (b - 1))
                for c in (0, 2):
                    act.activation(kd[:, par, :, :, c * D:(c + 1) * D], cx[:], ACT.Copy, scale=C_SCALE).then_inc(khi_ready, 1)

            def hi_x(b, last=False):
                act.wait_ge(nmr_ready, 2 * b + 3 - (1 if last else 0))
                if not is_first(b):
                    act.wait_ge(x_full, fills_r(b - 1) + 4)
                    act.wait_ge(pairs_out, 16 * b)
                for t in range(T2):
                    act.activation(xs[:, t, 0, :], x2[:, t], ACT.Identity, scale=rstd[:, 1, t:t + 1],
                                   bias=nmr[:, 1, t:t + 1]).then_inc(xhi_ready, 1)

            def k_stack(b, par):
                for u in range(2):
                    act.wait_ge(x_full, fills_p(b) + u + 1)
                    act.activation(ks[0:96, par, 4 * u:4 * u + 4, :].rearrange("p k s -> p (k s)"), ps_x16[0:96, :],
                                   ACT.Copy).then_inc(x_free, 1)

            def q_stack(b, par, kv):
                act.wait_ge(x_full, fill_q(b, kv) + 1)
                if kv == 0 and not (isinstance(b, int) and b < 2):
                    act.wait_ge(t_full, 16 * (b - 1))
                act.activation(qs[0:96, par, G * kv:G * kv + G, :].rearrange("p k s -> p (k s)"), ps_x16[0:96, :],
                               ACT.Copy).then_inc(x_free, 1)

            def m_rows(b, hf):
                act.wait_ge(x_full, fill_m(b, hf) + 1)
                if not is_first(b):
                    act.wait_ge(mrow_in[hf], 32 * b)
                act.activation(mrow[:, hf, :], ps_x16[0:32, 0:S], ACT.Copy).then_inc(x_free, 1)

            def x_stack(b):
                for u in range(4):
                    t, part = u // 2, u % 2
                    act.wait_ge(x_full, fills_r(b) + u + 1)
                    act.activation(xt[:, part, t].rearrange("p k s -> p (k s)"), ps_x16[:, :],
                                   ACT.Copy).then_inc(x_free, 1)

            def router_exp(b):
                act.wait_ge(lneg_ready, b + 1)
                for t in range(T2):
                    act.activation(lexp[:, t], lg[:, t], ACT.Exp, bias=lneg[:, t:t + 1],
                                   scale=1.0 / (XS_SCALE * W_SCALE)).then_inc(lexp_ready, 1)

            def exps(b, kv):
                for tt in range(2):
                    u = 2 * kv + tt
                    n = 16 * b + u
                    act.wait_ge(t_full, n + 1)
                    if not (isinstance(n, int) and n < 2):
                        act.wait_ge(plo_dve if tt == 0 else plo_pool, 8 * b + kv)
                    act.activation(prob[:, tt], ps_t[:, u % 2], ACT.Exp, bias=pbias[:],
                                   scale=1.0 / (XS_SCALE * C_SCALE * float(D) ** 0.5)).then_inc(t_free, 1)
                for tt in range(2):
                    u = 2 * kv + tt
                    n = 16 * b + u
                    act.wait_ge(t_free, n + 1)
                    if not (isinstance(n, int) and n < 4):
                        act.wait_ge(v_full, 8 * b + kv - 1)
                    act.activation(phi[:, u % 4], prob[:, tt], ACT.Copy).then_inc(phi_ready, 1)

            def step(b, par, last):
                for kv in range(KV):
                    exps(b, kv)
                    if kv == 0 and not is_first(b):
                        hi_x(b - 1)
                    if kv == 1 and not last:
                        hi_q(b + 1)
                        hi_k(b + 1, 1 - par)
                    if kv == 1 and not is_first(b):
                        x_stack(b - 1)
                    if kv == 2 and not is_first(b):
                        router_exp(b - 1)
                    if kv == 4 and not last:
                        k_stack(b + 1, 1 - par)
                    if kv == 7 and not last:
                        m_rows(b + 1, 0)
                    if kv >= 4 and not last:
                        q_stack(b + 1, 1 - par, 2 * kv - 8)
                        q_stack(b + 1, 1 - par, 2 * kv - 7)
                if not last:
                    m_rows(b + 1, 1)

            hi_q(0)
            hi_k(0, 0)
            k_stack(0, 0)
            for kv in range(KV):
                if kv == 6:
                    m_rows(0, 0)
                q_stack(0, 0, kv)
            m_rows(0, 1)
            loops(act, step)
            hi_x(nb - 1, True)
            x_stack(nb - 1)
            router_exp(nb - 1)
            act.wait_ge(lexp_ready, 2 * nb)
            act.activation(tgate[:, 0:1], pbias[:], ACT.Copy).then_inc(stage1, 1)
            act.wait_ge(stage1, 4)

            def split_hi(e, i):
                n = CHUNKS * e + i
                r = i % WRING
                act.wait_ge(w_in[r], 32 * (2 * e + i // WRING + 1))
                if i >= WRING:
                    act.wait_ge(gu_full, 2 * (FB * e + i - WRING + 1))
                elif not is_first(e):
                    if i == 0:
                        act.wait_ge(gu_full, 2 * FB * e)
                    else:
                        act.wait_ge(y_full, 8 * e - 8 + 4 * i)
                act.activation(wpair[:, r, 0], wraw[:, r], ACT.Copy, scale=W_SCALE).then_inc(wpair_hi, 1)

            def silu(e, j):
                n = FB * e + j
                act.wait_ge(gu_full, 2 * n + 1)
                if not (isinstance(n, int) and n < 2):
                    act.wait_ge(a32_ready, n - 1)
                act.activation(sg[:, j % 2], ps_gu[:, j % 2, 0], ACT.Silu, scale=1.0 / (XS_SCALE * W_SCALE)).then_inc(sg_ready, 1)

            def act_hi(e, j):
                n = FB * e + j
                act.wait_ge(a32_ready, n + 1)
                if not is_first(e) and j == 0:
                    act.wait_ge(y_full, 8 * e)
                act.activation(apair[:, 0, j], a32[:, j % 2], ACT.Copy).then_inc(ahi_ready, 1)

            def y_out(e, par, m):
                n, c = m // CT, m % CT
                act.wait_ge(y_full, 8 * e + m + 1)
                if not is_first(e) and n == 0 and c == 0:
                    act.wait_ge(added, 16 * CT * e)
                act.activation(ys[:, c, n * 512:(n + 1) * 512], ps_y[:, m % 2], ACT.Copy,
                               scale=slots[:, par, c, 1:2].bitcast(F32)).then_inc(y_free, 1)

            def step2(e, par, last):
                act.wait_ge(slots_in[par], 8 * e + 16 if par == 0 else 8 * (e + 1))
                for j in range(FB):
                    if j + 2 < CHUNKS:
                        split_hi(e, j + 2)
                    silu(e, j)
                    act_hi(e, j)
                for m in range(8):
                    if m == 0 and not last:
                        split_hi(e + 1, 0)
                    if m == 4 and not last:
                        split_hi(e + 1, 1)
                    y_out(e, par, m)

            split_hi(0, 0)
            split_hi(0, 1)
            loops2(act, step2)

        @block.vector
        def _(dve):
            setup = Tally(dve, dve_order)

            def link(ins, tally):
                tally.add(ins)
                tally.wait()

            dve.wait_ge(setup_act, 2)
            dve.tensor_scalar(tg_at[:], tgate[:, 0:1], 1.0 / C_SCALE, None, ALU.mult).then_inc(setup_dve, 1)
            dve.tensor_scalar(tg_ff[:], tgate[:, 1:2], ROUTE_SCALE / (A_SCALE * W_SCALE), None, ALU.mult).then_inc(setup_dve, 1)
            dve.scalar_tensor_tensor(out=wcpair[:, 1, :], in0=wcraw, scalar=W_SCALE, in1=wcpair[:, 0, :],
                                     op0=ALU.mult, op1=ALU.subtract).then_inc(setup_dve, 1)
            for u in range(2):
                dve.wait_ge(wc_t, u + 1)
                dve.tensor_copy(wc[:, :, u, :], ps_x16[:, 0:KB * NALL].rearrange("p (k e) -> p k e", k=KB)).then_inc(setup_dve, 1)
            dve.wait_ge(consts, 2)
            dve.wait_ge(setup_dve, 5)

            def carry_wait(tally):
                tally.add(dve.memset(spare[:, 0:1], 0.0))

            def norm_stats(src, which, tally):
                for t in range(T2):
                    for c in range(2):
                        tally.add(dve.bn_stats(stats[:, which, t, c], src[:, t, 512 * c:512 * c + 512]))
                tally.wait()
                carry_wait(tally)
                for t in range(T2):
                    tally.add(dve.bn_aggr(mv[:, which, t], stats[:, which, t]))
                tally.wait()
                scale = XS_SCALE ** -2
                dve.tensor_scalar(veps[:, which], mv[:, which, :, 1], scale, LN_EPS * scale, ALU.mult, ALU.add).then_inc(var_ready, 1)

            def norm_apply(src, which, n, tally):
                dve.wait_ge(rstd_ready, n)
                dve.scalar_tensor_tensor(out=nmr[:, which], in0=mv[:, which, :, 0], scalar=-1.0, in1=rstd[:, which],
                                         op0=ALU.mult, op1=ALU.mult).then_inc(nmr_ready, 1)
                dve.wait_ge(nmr_ready, n)
                for t in range(T2):
                    tally.add(dve.tensor_scalar(xn[:, t], src[:, t], rstd[:, which, t:t + 1], nmr[:, which, t:t + 1],
                                                ALU.mult, ALU.add))
                tally.wait()

            def stats_q(b, tally):
                dve.wait_ge(x1_in, 16 * (b + 1))
                norm_stats(x1, 0, tally)

            def low_q(b, tally):
                norm_apply(x1, 0, 1 if is_first(b) else 2 * b, tally)
                if not is_first(b):
                    dve.wait_ge(x_full, fill_q(b - 1, KV - 1) + 1)
                for t in range(T2):
                    dve.wait_ge(qhi_ready, 4 * b + 2 * t + 2)
                    ins = dve.tensor_tensor(qd[:, t, :, 2, :], xn[:, t].rearrange("p (h d) -> p h d", d=D),
                                            qd[:, t, :, 0, :], ALU.subtract)
                    if t == 0:
                        tally.add(ins)
                ins.then_inc(qd_ready, 1)

            def low_k(b, par):
                dve.wait_ge(khi_ready, 2 * b + 2)
                dve.scalar_tensor_tensor(out=kd[:, par, :, :, D:2 * D].rearrange("p t k d -> p (t k) d"),
                                         in0=cx[:].rearrange("p t k d -> p (t k) d"), scalar=C_SCALE,
                                         in1=kd[:, par, :, :, 0:D].rearrange("p t k d -> p (t k) d"),
                                         op0=ALU.mult, op1=ALU.subtract).then_inc(kd_ready, 1)

            def maxima(b, kv):
                for t in range(T2):
                    for pr in range(2):
                        n = 32 * b + 4 * kv + 2 * t + pr
                        dve.wait_ge(s_full, n + 1)
                        if kv == 0 and t == 0 and pr == 0 and not is_first(b):
                            dve.wait_ge(mpair_ready, 2 * b)
                        h = G * kv + 2 * pr
                        dve.tensor_reduce(mx[:, t, h:h + 2], ps_s[:, pr].rearrange("p (h s) -> p h s", h=2),
                                          AXX, ALU.max).then_inc(s_free, 1)

            def max_pairs(b, hf, tally):
                dve.wait_ge(s_free, 32 * b + 16 * (hf + 1))
                if not is_first(b):
                    dve.wait_ge(x_full, fill_m(b - 1, hf) + 1)
                src = mx[:, :, hf * 16:hf * 16 + 16]
                link(dve.tensor_scalar(mpair[:, hf, :, 0, :], src, -1.0 / M_SCALE, None, ALU.mult), tally)
                dve.scalar_tensor_tensor(out=mpair[:, hf, :, 1, :], in0=src, scalar=-1.0 / M_SCALE,
                                         in1=mpair[:, hf, :, 0, :], op0=ALU.mult, op1=ALU.subtract).then_inc(mpair_ready, 1)

            def low_probs(b, kv):
                u = 16 * b + 2 * kv
                dve.wait_ge(phi_ready, u + 1)
                if not (isinstance(u, int) and u < 4):
                    dve.wait_ge(v_full, 8 * b + kv - 1)
                r = (2 * kv) % 4
                dve.tensor_tensor(plo[:, r], prob[:, 0], phi[:, r], ALU.subtract).then_inc(plo_dve, 1)

            def heads_out(b, kv, tally):
                dve.wait_ge(v_full, 8 * b + kv + 1)
                link(dve.reciprocal(recip[:], ps_v[:, :, :, D]), tally)
                dve.tensor_tensor(at[:, :, G * kv:G * kv + G, :], ps_v[:, :, :, 0:D],
                                  recip[:].unsqueeze(3).to_broadcast([P, T2, G, D]), ALU.mult).then_inc(v_free, 1)

            def residual(b, tally, last=False):
                dve.wait_ge(xr_in, 16 * (b + 1))
                dve.wait_ge(v_free, 8 * (b + 1))
                if not is_first(b):
                    dve.wait_ge(x2_out, 16 * b)
                    dve.wait_ge(xs_ready, b)
                dve.scalar_tensor_tensor(out=x2[:].rearrange("p t h -> p (t h)"), in0=at[:].rearrange("p t h d -> p (t h d)"),
                                         scalar=tg_at[:], in1=xr[:].rearrange("p t h -> p (t h)"),
                                         op0=ALU.mult, op1=ALU.add).then_inc(x2_ready, 1)
                dve.wait_ge(x2_ready, b + 1)
                norm_stats(x2, 1, tally)

            def low_x(b, tally, last=False):
                norm_apply(x2, 1, 2 * b + 3 - (1 if last else 0), tally)
                for t in range(T2):
                    dve.wait_ge(xhi_ready, 2 * b + t + 1)
                    ins = dve.tensor_tensor(xs[:, t, 1], xn[:, t], xs[:, t, 0], ALU.subtract)
                    if t == 0:
                        tally.add(ins)
                ins.then_inc(xs_ready, 1)

            def bc(ap, shape):
                return ap.to_broadcast(shape)

            def router_a(b, tally):
                dve.wait_ge(x_full, fills_r(b) + 5)
                dve.tensor_reduce(lg[:], ps_x[:, 0:2 * T2 * NALL].rearrange("p (t a e) -> p t e a", t=T2, a=2),
                                  AXX, ALU.add).then_inc(x_free, 1)
                dve.wait_ge(x_free, fills_r(b) + 5)
                link(dve.tensor_reduce(lmax[:], lg[:], AXX, ALU.max), tally)
                dve.tensor_scalar(lneg[:], lmax[:], -1.0 / (XS_SCALE * W_SCALE), None, ALU.mult).then_inc(lneg_ready, 1)

            def router_b(b, tally):
                dve.wait_ge(lexp_ready, 2 * b + 2)
                link(dve.tensor_reduce(lsum[:], lexp[:], AXX, ALU.add), tally)
                link(dve.reciprocal(lrec[:], lsum[:]), tally)
                link(dve.tensor_tensor(score[:], lexp[:], bc(lrec[:].unsqueeze(2), [P, T2, NALL]), ALU.mult), tally)
                link(dve.tensor_tensor(biased[:], score[:], bc(bias_b[:].unsqueeze(1), [P, T2, NALL]), ALU.add), tally)
                carry_wait(tally)
                for t in range(T2):
                    tally.add(dve.max(top[:, t], biased[:, t]))
                tally.wait()
                carry_wait(tally)
                for t in range(T2):
                    tally.add(dve.max_index(topi[:, t], top[:, t], biased[:, t]))
                    tally.add(dve.match_replace(left[:, t], top[:, t], biased[:, t], -1e30))
                tally.wait()
                dve.tensor_tensor(mask[:], left[:], biased[:], ALU.not_equal).then_inc(mask_ready, 1)
                tally.add(dve.tensor_copy(topf[:], topi[:]))
                dve.wait_ge(mask_ready, b + 1)
                link(dve.tensor_tensor(wsel[:], score[:], mask[:], ALU.mult), tally)
                tally.add(dve.tensor_reduce(wsum[:, :, 0], wsel[:], AXX, ALU.add))
                tally.add(dve.tensor_reduce(wzero[:, :, 0], wsel[:, :, NROUTED:], AXX, ALU.add))
                tally.add(dve.tensor_tensor(hot[:].rearrange("p t k e -> p (t k) e"),
                                            bc(iota_e[:].unsqueeze(1), [P, T2 * TOPK, NROUTED]),
                                            bc(topf[:].rearrange("p t k -> p (t k)").unsqueeze(2), [P, T2 * TOPK, NROUTED]),
                                            ALU.is_equal))
                tally.wait()
                link(dve.tensor_scalar(wsum[:], wsum[:], ROUTE_EPS, None, ALU.add), tally)
                link(dve.reciprocal(wrec[:], wsum[:]), tally)
                link(dve.tensor_tensor(wzero[:], wzero[:], wrec[:], ALU.mult), tally)
                link(dve.tensor_scalar(wzero[:], wzero[:], ROUTE_SCALE, 1.0, ALU.mult, ALU.add), tally)
                link(dve.scalar_tensor_tensor(out=wfac[:, :, 0], in0=wzero[:, :, 0], scalar=tg_ff[:], in1=wrec[:, :, 0],
                                              op0=ALU.mult, op1=ALU.mult), tally)
                link(dve.tensor_tensor(coef[:], wsel[:, :, 0:NROUTED], bc(wfac[:], [P, T2, NROUTED]), ALU.mult), tally)

            def router_c(b, tally):
                dve.wait_ge(x_full, fills_r(b) + 6)
                px = ps_x[:, 0:3 * NROUTED].rearrange("p (t e) -> p t e", t=3)
                link(dve.tensor_tensor(pos[:], px[:, 0:2], bc(carry[:].unsqueeze(1), [P, T2, NROUTED]), ALU.add), tally)
                dve.tensor_tensor(carry[:], px[:, 2], carry[:], ALU.add).then_inc(x_free, 1)
                link(dve.tensor_tensor(place[:], pos[:], bc(slot0[:].unsqueeze(1), [P, T2, NROUTED]), ALU.add), tally)
                link(dve.scalar_tensor_tensor(out=place[:], in0=pos[:], scalar=float(CAP), in1=place[:],
                                              op0=ALU.is_lt, op1=ALU.mult), tally)
                for w, src in ((0, place), (1, coef)):
                    for t in range(T2):
                        tally.add(dve.tensor_tensor(pick[:, w, t], hot[:, t], bc(src[:, t].unsqueeze(1), [P, TOPK, NROUTED]), ALU.mult))
                tally.wait()
                link(dve.tensor_reduce(picked[:], pick[:].rearrange("p w t k e -> p w (t k) e"), AXX, ALU.add), tally)
                if not is_first(b):
                    dve.wait_ge(lists_out, 16 * T2 * TOPK * b)
                tally.add(dve.tensor_scalar(dest[:], picked[:, 0], NO_SLOT, None, ALU.add))
                tally.add(dve.tensor_copy(entry[:, :, 1].bitcast(F32), picked[:, 1]))
                link(dve.tensor_copy(entry[:, :, 0], token[:].rearrange("p t k -> p (t k)")), tally)
                dve.tensor_scalar(token[:], token[:], float(S), None, ALU.add).then_inc(entry_ready, 1)
                dve.wait_ge(entry_ready, b + 1)

            N_RES, N_LOWX, N_RA, N_RB, N_RC = 7, 3, 1, 23, 11
            N_R = N_RES + N_LOWX + N_RA + N_RB + N_RC
            N_P = 7 + 3 + 2
            N_V = KV

            def orders(b):
                if is_first(b):
                    return N_P
                return N_P + (N_P + N_V) + (N_P + N_V + N_R) * (b - 1)

            def step(b, par, last):
                tally = Tally(dve, dve_order, orders(b))
                for kv in range(KV):
                    if kv == 0 and not is_first(b):
                        residual(b - 1, tally)
                    low_probs(b, kv)
                    if kv == 0 and not is_first(b):
                        low_x(b - 1, tally)
                    if kv == 0 and not last:
                        stats_q(b + 1, tally)
                    if kv == 1 and not last:
                        low_q(b + 1, tally)
                        low_k(b + 1, 1 - par)
                    if kv > 0:
                        heads_out(b, kv - 1, tally)
                    if kv == 2 and not is_first(b):
                        router_a(b - 1, tally)
                    if kv == 3 and not is_first(b):
                        router_b(b - 1, tally)
                    if kv == 4 and not is_first(b):
                        router_c(b - 1, tally)
                    if kv >= 4 and not last:
                        maxima(b + 1, 2 * kv - 8)
                        maxima(b + 1, 2 * kv - 7)
                    if kv == 6 and not last:
                        max_pairs(b + 1, 0, tally)
                if not last:
                    max_pairs(b + 1, 1, tally)
                heads_out(b, KV - 1, tally)
                tally.close((0 if last else N_P) + N_V + (0 if is_first(b) else N_R))

            tally = Tally(dve, dve_order, 0)
            stats_q(0, tally)
            low_q(0, tally)
            low_k(0, 0)
            for kv in range(KV):
                maxima(0, kv)
                if kv == 3:
                    max_pairs(0, 0, tally)
            max_pairs(0, 1, tally)
            tally.close(N_P)
            loops(dve, step)
            tally = Tally(dve, dve_order, orders(nb - 1) + N_V + N_R)
            residual(nb - 1, tally)
            low_x(nb - 1, tally, True)
            router_a(nb - 1, tally)
            router_b(nb - 1, tally)
            router_c(nb - 1, tally)
            dve.wait_ge(x_free, fills_r(nb - 1) + 6)
            dve.tensor_copy(filled[:], carry[0:1, :]).then_inc(stage1, 1)
            dve.wait_ge(stage1, 4)

            def split_lo(e, i):
                n = CHUNKS * e + i
                r = i % WRING
                dve.wait_ge(wpair_hi, n + 1)
                dve.scalar_tensor_tensor(out=wpair[:, r, 1], in0=wraw[:, r], scalar=W_SCALE, in1=wpair[:, r, 0],
                                         op0=ALU.mult, op1=ALU.subtract).then_inc(wpair_lo, 1)

            def take_t(e, par, u):
                c, part = u // 2, u % 2
                dve.wait_ge(gt_full, 8 * e + u + 1)
                dve.tensor_copy(xgt[:, par, part, :, c * P:(c + 1) * P],
                                ps_g16[u % 2].rearrange("p (k t) -> p k t", k=KB)).then_inc(gt_free, 1)

            def gate_up(e, j):
                n = FB * e + j
                dve.wait_ge(gu_full, 2 * n + 2)
                dve.wait_ge(sg_ready, n + 1)
                if not (isinstance(n, int) and n < 2):
                    dve.wait_ge(alo_ready, n - 1)
                dve.scalar_tensor_tensor(out=a32[:, j % 2], in0=ps_gu[:, j % 2, 1],
                                         scalar=A_SCALE / (XS_SCALE * W_SCALE), in1=sg[:, j % 2],
                                         op0=ALU.mult, op1=ALU.mult).then_inc(a32_ready, 1)

            def act_lo(e, j):
                n = FB * e + j
                dve.wait_ge(ahi_ready, n + 1)
                dve.tensor_tensor(apair[:, 1, j], a32[:, j % 2], apair[:, 0, j], ALU.subtract).then_inc(alo_ready, 1)

            def step2(e, par, last):
                for j in range(FB):
                    if j + 2 < CHUNKS:
                        split_lo(e, j + 2)
                    gate_up(e, j)
                    act_lo(e, j)
                if not last:
                    for u in range(8):
                        take_t(e + 1, 1 - par, u)
                    split_lo(e + 1, 0)
                    split_lo(e + 1, 1)

            for u in range(8):
                take_t(0, 0, u)
            split_lo(0, 0)
            split_lo(0, 1)
            loops2(dve, step2)

        @block.tensor
        def _(pe):
            pe.wait_ge(consts, 2)
            pe.wait_ge(setup_act, 2)
            pe.wait_ge(setup_dve, 3)
            for u in range(2):
                if u:
                    pe.wait_ge(setup_dve, 4)
                for k in range(KB):
                    mm = pe.transpose(ps_x16[:, k * NALL:(k + 1) * NALL], wcpair[:, u, k * P:(k + 1) * P], ident[0:NALL, 0:NALL])
                mm.then_inc(wc_t, 1)
            pe.wait_ge(setup_dve, 5)

            def take_bank(n):
                if not (isinstance(n, int) and n == 0):
                    pe.wait_ge(x_free, n)

            def k_transpose(b, par):
                pe.wait_ge(kd_ready, b + 1)
                for u in range(2):
                    take_bank(fills_p(b) + u)
                    for k in range(4):
                        for t in range(T2):
                            mm = pe.transpose(ps_x16[0:96, k * S + t * P:k * S + (t + 1) * P], kd[:, par, t, 4 * u + k, 0:96], ident[:])
                    mm.then_inc(x_full, 1)

            def q_transpose(b, kv):
                if kv == 0:
                    pe.wait_ge(qd_ready, b + 1)
                take_bank(fill_q(b, kv))
                for g in range(G):
                    for t in range(T2):
                        mm = pe.transpose(ps_x16[0:96, g * S + t * P:g * S + (t + 1) * P],
                                          qd[:, t, G * kv + g].rearrange("p c d -> p (c d)"), ident[:])
                mm.then_inc(x_full, 1)

            def m_transpose(b, hf):
                pe.wait_ge(mpair_ready, 2 * b + hf + 1)
                take_bank(fill_m(b, hf))
                for t in range(T2):
                    mm = pe.transpose(ps_x16[0:32, t * P:(t + 1) * P], mpair[:, hf, t].rearrange("p a h -> p (a h)"), ident[:])
                mm.then_inc(x_full, 1)

            def scores(b, par, kv):
                n_x = fill_q(b, kv) + 1
                pe.wait_ge(x_free, n_x)
                for t in range(T2):
                    for pr in range(2):
                        n = 32 * b + 4 * kv + 2 * t + pr
                        if not (isinstance(n, int) and n < 2):
                            pe.wait_ge(s_free, n - 1)
                        for i in range(2):
                            h = G * kv + 2 * pr + i
                            mm = pe.matmul(ps_s[:, pr, i * S:(i + 1) * S], qs[0:96, par, h, t * P:(t + 1) * P],
                                           ks[0:96, par, kv, :], start=True, stop=True)
                        mm.then_inc(s_full, 1)

            def scores_t(b, par, kv):
                if kv % 4 == 0:
                    pe.wait_ge(mrow_in[kv // 4], 32 * (b + 1))
                for tt in range(2):
                    n = 16 * b + 2 * kv + tt
                    if not (isinstance(n, int) and n < 2):
                        pe.wait_ge(t_free, n - 1)
                    for pr in range(2):
                        h = G * kv + 2 * pr
                        mm = pe.matmul(ps_t[:, tt, 512 * pr:512 * pr + 512], ks[0:98, par, kv, tt * P:(tt + 1) * P],
                                       qs[0:98, par, h:h + 2, :], start=True, stop=True)
                    mm.then_inc(t_full, 1)

            def values(b, par, kv):
                pe.wait_ge(plo_dve, 8 * b + kv + 1)
                pe.wait_ge(plo_pool, 8 * b + kv + 1)
                n = 8 * b + kv
                if not (isinstance(n, int) and n == 0):
                    pe.wait_ge(v_free, n)
                for t in range(T2):
                    for g in range(G):
                        c0 = g * S + t * P
                        for tt in range(2):
                            r = (2 * kv + tt) % 4
                            pe.matmul(ps_v[:, t, g, :], phi[:, r, c0:c0 + P], kd[:, par, tt, kv, 64:97],
                                      start=(tt == 0), stop=False)
                            pe.matmul(ps_v[:, t, g, 0:D], phi[:, r, c0:c0 + P], kd[:, par, tt, kv, D:2 * D],
                                      start=False, stop=False)
                            mm = pe.matmul(ps_v[:, t, g, :], plo[:, r, c0:c0 + P], kd[:, par, tt, kv, 64:97],
                                           start=False, stop=(tt == 1))
                mm.then_inc(v_full, 1)

            def x_transpose(b, us):
                for u in us:
                    t, part = u // 2, u % 2
                    if u == 0:
                        pe.wait_ge(xs_ready, b + 1)
                    take_bank(fills_r(b) + u)
                    for k in range(KB):
                        mm = pe.transpose(ps_x16[:, k * P:(k + 1) * P], xs[:, t, part, k * P:(k + 1) * P], ident[:])
                    mm.then_inc(x_full, 1)

            def logits(b):
                take_bank(fills_r(b) + 4)
                for t in range(T2):
                    for part in range(2):
                        for k in range(KB):
                            mm = pe.matmul(ps_x[:, t * 2 * NALL:(t + 1) * 2 * NALL], xt[:, part, t, k, :],
                                           wc[:, k].rearrange("p a e -> p (a e)"), start=(part == 0 and k == 0),
                                           stop=(part == 1 and k == KB - 1))
                mm.then_inc(x_full, 1)

            def counts(b):
                pe.wait_ge(mask_ready, b + 1)
                take_bank(fills_r(b) + 5)
                m0, m1 = mask[:, 0, 0:NROUTED], mask[:, 1, 0:NROUTED]
                n = NROUTED
                pe.matmul(ps_x[:, 0:n], tri[:], m0, start=True, stop=True)
                pe.matmul(ps_x[:, n:2 * n], ones[:], m0, start=True, stop=False)
                pe.matmul(ps_x[:, n:2 * n], tri[:], m1, start=False, stop=True)
                pe.matmul(ps_x[:, 2 * n:3 * n], ones[:], m0, start=True, stop=False)
                pe.matmul(ps_x[:, 2 * n:3 * n], ones[:], m1, start=False, stop=True).then_inc(x_full, 1)

            def step(b, par, last):
                for kv in range(KV):
                    scores_t(b, par, kv)
                    if kv == 1 and not is_first(b):
                        x_transpose(b - 1, range(4))
                    if kv == 2 and not is_first(b):
                        logits(b - 1)
                    if kv > 0:
                        values(b, par, kv - 1)
                    if kv == 4 and not is_first(b):
                        counts(b - 1)
                    if kv == 4 and not last:
                        k_transpose(b + 1, 1 - par)
                    if kv >= 4 and not last:
                        if kv == 7:
                            m_transpose(b + 1, 0)
                        q_transpose(b + 1, 2 * kv - 8)
                        scores(b + 1, 1 - par, 2 * kv - 8)
                        q_transpose(b + 1, 2 * kv - 7)
                        scores(b + 1, 1 - par, 2 * kv - 7)
                values(b, par, KV - 1)
                if not last:
                    m_transpose(b + 1, 1)

            k_transpose(0, 0)
            for kv in range(KV):
                if kv == 6:
                    m_transpose(0, 0)
                q_transpose(0, kv)
                scores(0, 0, kv)
            m_transpose(0, 1)
            loops(pe, step)
            x_transpose(nb - 1, range(4))
            logits(nb - 1)
            counts(nb - 1)
            pe.wait_ge(x_free, fills_r(nb - 1) + 6)
            pe.transpose(ps_x16[0:32, 0:P], ident[:, 0:32], ident[:]).then_inc(stage1, 1)
            pe.wait_ge(stage1, 4)

            def t_rows(e, us):
                for u in us:
                    c, part = u // 2, u % 2
                    if u == 0:
                        pe.wait_ge(gathered, 16 * CT * (e + 1))
                    n = 8 * e + u
                    if not (isinstance(n, int) and n < 2):
                        pe.wait_ge(gt_free, n - 1)
                    for k in range(KB):
                        mm = pe.transpose(ps_g16[u % 2][:, k * P:(k + 1) * P], xg[:, c, part, k * P:(k + 1) * P], ident[:])
                    mm.then_inc(gt_full, 1)

            TERMS = ((0, 0), (0, 1), (1, 0))

            def up(e, par, j, nt):
                n = FB * e + j
                pe.wait_ge(wpair_lo, CHUNKS * e + j + 1)
                if not (isinstance(n, int) and n < 2):
                    pe.wait_ge(a32_ready, n - 1)
                w = wpair[:, j % WRING].rearrange("p a (k h f) -> p a k h f", k=KB, h=2)
                for h in range(2):
                    for k in range(KB):
                        for a, c in TERMS:
                            mm = pe.matmul(ps_gu[:, j % 2, h, 0:nt * P], w[:, a, k, h, :], xgt[:, par, c, k, 0:nt * P],
                                           start=(k == 0 and (a, c) == (0, 0)), stop=(k == KB - 1 and a == 1))
                    mm.then_inc(gu_full, 1)

            def down(e, n2, nt):
                i = FB + n2
                pe.wait_ge(wpair_lo, CHUNKS * e + i + 1)
                pe.wait_ge(alo_ready, FB * (e + 1))
                w = wpair[:, i % WRING].rearrange("p a (k h) -> p a k h", k=FB)
                for c in range(CT):
                    m = CT * n2 + c
                    n = 8 * e + m
                    if not (isinstance(n, int) and n < 2):
                        pe.wait_ge(y_free, n - 1)
                    if c >= nt:
                        pe.matmul(ps_y[:, m % 2, 0:2], ident[:], ident[:, 0:2], start=True, stop=True).then_inc(y_full, 1)
                        continue
                    for k in range(FB):
                        for a, o in ((0, 0), (1, 0), (0, 1)):
                            mm = pe.matmul(ps_y[:, m % 2], apair[:, o, k, c * P:(c + 1) * P], w[:, a, k, :],
                                           start=(k == 0 and (a, o) == (0, 0)), stop=(k == FB - 1 and o == 1))
                    mm.then_inc(y_full, 1)

            def products(e, par, last, nt):
                for j in range(FB):
                    up(e, par, j, nt)
                if not last:
                    t_rows(e + 1, range(8))
                for n2 in range(2):
                    down(e, n2, nt)

            def step2(e, par, last):
                if is_first(e):
                    products(e, par, last, CT)
                    return
                n = pe.value_load(filled[0:1, bass.ds(e, 1)], min_val=0, max_val=ntok)
                with pe.If(n < 2 * P + 1):
                    with pe.If(n < P + 1):
                        products(e, par, last, 1)
                    with pe.Else():
                        products(e, par, last, 2)
                with pe.Else():
                    with pe.If(n < 3 * P + 1):
                        products(e, par, last, 3)
                    with pe.Else():
                        products(e, par, last, 4)

            t_rows(0, range(8))
            pe.wait_ge(gt_free, 8)
            loops2(pe, step2)


_INS = ['x', 'ctx_512', 'g_xattn', 'g_ffn', 'L0_ffn_w_cls', 'L0_ffn_bias', 'L0_ffn_w_gate_up', 'L0_ffn_w_down']
_OUTS = [((16, 256, 1024), 'float32')]


def kernel(**inputs):
    import numpy as _np
    import concourse.bacc as _bacc
    from concourse import mybir as _mybir
    from concourse.bass_utils import run_bass_kernel_spmd as _run

    nc = _bacc.Bacc("TRN2", target_bir_lowering=False, num_devices=1)
    arrays, args = {}, []
    for name in _INS:
        a = _np.ascontiguousarray(inputs[name])
        arrays[f"in_{name}_dram"] = a
        args.append(nc.dram_tensor(f"in_{name}_dram", a.shape, _mybir.dt.from_np(a.dtype), kind="ExternalInput").ap())
    for i, (shape, dtype) in enumerate(_OUTS):
        dt = _mybir.dt.from_np(_np.dtype(dtype))
        args.append(nc.dram_tensor(f"out_{i}_dram", shape, dt, kind="ExternalOutput").ap())
    gated_block_kernel(nc, *args)
    r = _run(nc, [arrays], core_ids=[0])
    return r.results[0]["out_0_dram"]
```

```python
from contextlib import ExitStack

import concourse.bass as bass
from concourse import mybir

F32 = mybir.dt.float32
F16 = mybir.dt.float16
I32 = mybir.dt.int32
U32 = mybir.dt.uint32
ALU = mybir.AluOpType
ACT = mybir.ActivationFunctionType
AXX = mybir.AxisListType.X

P = 128
D = 32
G = 4
KV = 8
NH = G * KV
S = 256
T2 = S // P
H = NH * D
KB = H // P
NROUTED = 32
NALL = 64
TOPK = 8
CAP = 512
CT = CAP // P
FF = 512
FB = FF // P
ROUTE_SCALE = 1.5
LN_EPS = 1e-5
ROUTE_EPS = 1e-20

XS_SCALE = 64.0
C_SCALE = 16.0
W_SCALE = 256.0
A_SCALE = 32.0
M_SCALE = 32768.0
P_LOG = 12
NO_SLOT = float(1 << 20)


FILLS_AHEAD = ["K0", "K1", "Q0", "Q1", "Q2", "Q3", "M0", "Q4", "Q5", "Q6", "Q7"]
FILLS = ["K0", "K1", "Q0", "M1", "Q1", "Q2", "X0", "X1", "X2", "X3", "Q3", "M0", "Q4", "L", "Q5", "Q6", "C", "Q7"]
FILLS_FIRST = [f for f in FILLS if f[0] not in "XLC"]
FILLS_LAST = [f for f in FILLS if f[0] in "XLC" or f == "M1"]
FILLS_BEHIND = [f for f in FILLS if f[0] in "XLC"]
CHUNKS = FB + 2
WRING = 3


class Tally:

    def __init__(self, engine, sem, base=0):
        self.engine, self.sem, self.base, self.n = engine, sem, base, 0

    def add(self, instruction):
        instruction.then_inc(self.sem, 1)
        self.n += 1
        return self.base + self.n

    def wait(self, value=None):
        self.engine.wait_ge(self.sem, self.base + self.n if value is None else value)

    def close(self, steps):
        assert self.n == steps, (self.n, steps)


def gated_block_kernel(nc, x, ctx_512, g_xattn, g_ffn, w_cls, bias, w_gate_up, w_down, out, nb=16, ne=NROUTED):
    ntok = nb * S
    x_v = x.rearrange("b (t p) h -> b p t h", p=P)
    c_v = ctx_512.rearrange("b (t p) h -> b p t h", p=P)
    o_v = out.rearrange("b (t p) h -> b p t h", p=P)
    o_rows = out.rearrange("b s h -> (b s) h")
    gu_v = w_gate_up.rearrange("e (k p) (h f) -> e p k h f", p=P, h=2)
    dn_v = w_down.rearrange("e (k p) h -> e p k h", p=P)
    pairs = nc.dram_tensor("pairs", [ntok, 2 * H], F16).ap()
    lists = nc.dram_tensor("lists", [NROUTED * CAP, 2], I32).ap()
    pairs_v = pairs.rearrange("(b t p) h -> b p t h", p=P, t=T2)
    lists_v = lists.rearrange("(e c p) w -> e p c w", p=P, c=CT)
    lists_all = lists.rearrange("(p a) w -> p (a w)", p=P)

    with ExitStack() as whole:
        stack = [whole]

        def sb(name, shape, dt=F32):
            return stack[-1].enter_context(nc.sbuf_tensor(name, shape, dt))

        def sem(name):
            return whole.enter_context(nc.semaphore(name))

        psum = whole.enter_context(nc.psum_tensor("psum", [P, 8, 512], F32))

        ident = sb("ident", [P, P], F16)
        spare = sb("spare", [P, 4])
        filled = sb("filled", [1, NROUTED], I32)

        first = ExitStack()
        stack.append(first)
        qd = sb("qd", [P, 2, T2, NH, 3, D], F16)
        qs = sb("qs", [98, 2, NH, S], F16)
        x1 = sb("x1", [P, T2, H])
        xr = sb("xr", [P, T2, H])
        xn = sb("xn", [P, T2, H])
        cx = sb("cx", [P, T2, KV, D])
        kd = sb("kd", [P, T2, KV, 98], F16)
        vd = sb("vd", [P, 2, T2, KV, 98], F16)
        ks = sb("ks", [98, 2, KV, S], F16)
        mx = sb("mx", [P, T2, NH])
        mpair = sb("mpair", [P, 2, T2, 2, NH // 2], F16)
        mrow = sb("mrow", [32, 2, S], F16)
        prob = sb("prob", [P, 4, G * S])
        phi = sb("phi", [P, 8, G * S], F16)
        plo = sb("plo", [P, 8, G * S], F16)
        at = sb("at", [P, T2, NH, D])
        x2 = sb("x2", [P, T2, H])
        xs = sb("xs", [P, T2, 2, H], F16)
        xt = sb("xt", [P, 2, T2, KB, P], F16)
        wc = sb("wc", [P, KB, 2, NALL], F16)
        stats = sb("stats", [P, 2, T2, 2, 6])
        mv = sb("mv", [P, 2, T2, 2])
        veps = sb("veps", [P, 2, T2])
        rstd = sb("rstd", [P, 2, T2])
        nmr = sb("nmr", [P, 2, T2])
        half = sb("half", [P, T2])
        pbias = sb("pbias", [P, 1])
        recip = sb("recip", [P, T2, G])
        gates = sb("gates", [P, 2])
        tgate = sb("tgate", [P, 2])
        tg_at = sb("tg_at", [P, 1])
        tg_ff = sb("tg_ff", [P, 1])
        bias_b = sb("bias_b", [P, NALL])
        tri = sb("tri", [P, P], F16)
        ones = sb("ones", [P, P], F16)
        iota_e = sb("iota_e", [P, NROUTED])
        slot0 = sb("slot0", [P, NROUTED])
        token = sb("token", [P, T2, TOPK])
        lg = sb("lg", [P, T2, NALL])
        lmax = sb("lmax", [P, T2])
        lneg = sb("lneg", [P, T2])
        lexp = sb("lexp", [P, T2, NALL])
        lsum = sb("lsum", [P, T2])
        lrec = sb("lrec", [P, T2])
        score = sb("score", [P, T2, NALL])
        biased = sb("biased", [P, T2, NALL])
        top = sb("top", [P, T2, TOPK])
        topi = sb("topi", [P, T2, TOPK], U32)
        topf = sb("topf", [P, T2, TOPK])
        left = sb("left", [P, T2, NALL])
        mask = sb("mask", [P, T2, NALL], F16)
        wsel = sb("wsel", [P, T2, NALL])
        wsum = sb("wsum", [P, T2, 1])
        wzero = sb("wzero", [P, T2, 1])
        wrec = sb("wrec", [P, T2, 1])
        wfac = sb("wfac", [P, T2, 1])
        coef = sb("coef", [P, T2, NROUTED])
        pos = sb("pos", [P, T2, NROUTED])
        place = sb("place", [P, T2, NROUTED])
        carry = sb("carry", [P, NROUTED])
        hot = sb("hot", [P, T2, TOPK, NROUTED])
        pick = sb("pick", [P, 2, T2, TOPK, NROUTED])
        picked = sb("picked", [P, 2, T2 * TOPK])
        dest = sb("dest", [P, T2 * TOPK], I32)
        entry = sb("entry", [P, T2 * TOPK, 2], I32)
        wcraw = at[0:NALL, 0].rearrange("p h d -> p (h d)")
        wcpair = phi[0:NALL, 0:2, :]
        empty = sb("empty", [P, NROUTED * CT, 2], I32)
        stack.pop()
        first.close()

        wraw = sb("wraw", [P, WRING, 2048])
        wpair = sb("wpair", [P, WRING, 2, 2048], F16)
        xg = sb("xg", [P, CT, 2, H], F16)
        xgt = sb("xgt", [P, 2, 2, KB, CAP], F16)
        slots = sb("slots", [P, 2, CT, 2], I32)
        sg = sb("sg", [P, 2, CAP])
        a32 = sb("a32", [P, 2, CAP])
        apair = sb("apair", [P, 2, FB, CAP], F16)
        ys = sb("ys", [P, CT, H])

        ps_s = psum[:, 0:2, :]
        ps_t = psum[:, 2:6, :].rearrange("p (r b) n -> p r (b n)", r=2)
        ps_v = psum[:, 6, 0:T2 * G * 33].rearrange("p (t g d) -> p t g d", t=T2, g=G)
        ps_x = psum[:, 7, :]
        ps_x16 = psum[:, 7, :].bitcast(F16)
        ps_gu = psum[:, 0:4, :].rearrange("p (r h) n -> p r h n", r=2)
        ps_y = psum[:, 4:6, :]
        ps_g16 = [psum[:, 6, :].bitcast(F16), psum[:, 7, :].bitcast(F16)]

        small_in = sem("small_in")
        x1_in, cx_in, xr_in = sem("x1_in"), sem("cx_in"), sem("xr_in")
        mrow_in = [sem("mrow_in0"), sem("mrow_in1")]
        x2_out, pairs_out = sem("x2_out"), sem("pairs_out")
        lists_set, lists_out = sem("lists_set"), sem("lists_out")
        w_in = [sem(f"w_in{i}") for i in range(WRING)]
        slots_in = [sem("slots_in0"), sem("slots_in1")]
        gathered = sem("gathered")
        added = sem("added")
        consts = sem("consts")
        dve_order = sem("dve_order")
        pool_order = sem("pool_order")
        setup_dve = sem("setup_dve")
        setup_act = sem("setup_act")
        wc_t = sem("wc_t")
        var_ready = sem("var_ready")
        rstd_ready = sem("rstd_ready")
        nmr_ready = sem("nmr_ready")
        qhi_ready = sem("qhi_ready")
        xn_ready = sem("xn_ready")
        qlo_ready = sem("qlo_ready")
        vd_ready = sem("vd_ready")
        khi_ready = sem("khi_ready")
        kd_ready = sem("kd_ready")
        x_full, x_free = sem("x_full"), sem("x_free")
        s_full, s_free = sem("s_full"), sem("s_free")
        stack_ready = sem("stack_ready")
        mpair_ready = sem("mpair_ready")
        t_full, t_free = sem("t_full"), sem("t_free")
        phi_dve, phi_act = sem("phi_dve"), sem("phi_act")
        plo_dve, plo_pool = sem("plo_dve"), sem("plo_pool")
        v_full, v_free = sem("v_full"), sem("v_free")
        x2_ready = sem("x2_ready")
        xhi_ready = sem("xhi_ready")
        xs_ready = sem("xs_ready")
        lneg_ready, lexp_ready = sem("lneg_ready"), sem("lexp_ready")
        mask_ready = sem("mask_ready")
        entry_ready = sem("entry_ready")
        stage1 = sem("stage1")
        wpair_hi, wpair_lo = sem("wpair_hi"), sem("wpair_lo")
        gt_full, gt_free = sem("gt_full"), sem("gt_free")
        gu_full = sem("gu_full")
        sg_ready, a32_ready = sem("sg_ready"), sem("a32_ready")
        ahi_ready, alo_ready = sem("ahi_ready"), sem("alo_ready")
        y_full, y_free = sem("y_full"), sem("y_free")

        def nth_fill(step, name):
            if not isinstance(step, int):
                return len(FILLS_AHEAD) + len(FILLS_FIRST) + len(FILLS) * (step - 1) + FILLS.index(name) + 1
            if step == -1:
                return FILLS_AHEAD.index(name) + 1
            if step == 0:
                return len(FILLS_AHEAD) + FILLS_FIRST.index(name) + 1
            base = len(FILLS_AHEAD) + len(FILLS_FIRST) + len(FILLS) * (step - 1)
            if step < nb - 1:
                return base + FILLS.index(name) + 1
            if step == nb - 1:
                return base + FILLS_LAST.index(name) + 1
            return base - len(FILLS) + len(FILLS_LAST) + FILLS_BEHIND.index(name) + 1

        def of_p(b, name):
            return nth_fill(b - 1, name)

        def of_r(b, name):
            return nth_fill(b + 1, name)

        def fill_m(b, hf):
            return nth_fill(b, "M1") if hf else of_p(b, "M0")

        def nth_norm1(b):
            return b + 1 if isinstance(b, int) and b < 2 else 2 * b - 1

        def nth_norm2(b):
            return 2 * b + 4 - (max(0, b - (nb - 3)) if isinstance(b, int) else 0)

        def loops(eng, step):
            step(0, 0)
            step(1, 1)
            with eng.Fori(0, (nb - 4) // 2) as i:
                step(2 * i + 2, 0)
                step(2 * i + 3, 1)
            step(nb - 2, 0)
            step(nb - 1, 1)

        def has_r(b):
            return not is_first(b)

        def has_p(b):
            return not (isinstance(b, int) and b == nb - 1)

        def has_a(b):
            return not (isinstance(b, int) and b >= nb - 2)

        def loops2(eng, step):
            step(0, 0, False)
            with eng.Fori(0, (ne - 2) // 2) as i:
                step(2 * i + 1, 1, False)
                step(2 * i + 2, 0, False)
            step(ne - 1, 1, True)

        def is_first(b):
            return isinstance(b, int) and b == 0


        block = whole.enter_context(nc.Block())

        @block.sync
        def _(sp):
            sp.dma_start(gates[:, 0:1], g_xattn.rearrange("(a b) -> a b", a=1).to_broadcast([P, 1])).then_inc(small_in, 16)
            sp.dma_start(gates[:, 1:2], g_ffn.rearrange("(a b) -> a b", a=1).to_broadcast([P, 1])).then_inc(small_in, 16)
            sp.dma_start(bias_b[:], bias.rearrange("(a b) -> a b", a=1).to_broadcast([P, NALL])).then_inc(small_in, 16)
            sp.dma_start(wcraw, w_cls).then_inc(small_in, 16)
            sp.dma_start(x1[:], x_v[0]).then_inc(x1_in, 16)
            sp.dma_start(cx[:], c_v[0].rearrange("p t (k d) -> p t k d", d=D)).then_inc(cx_in, 16)
            sp.wait_ge(consts, 1)
            sp.dma_start(lists_all, empty[:].rearrange("p a w -> p (a w)")).then_inc(lists_set, 16)

            def load_a(b):
                if not is_first(b):
                    sp.wait_ge(qlo_ready, 2 * b)
                    sp.wait_ge(kd_ready, b)
                sp.dma_start(x1[:], x_v[b]).then_inc(x1_in, 16)
                sp.dma_start(cx[:], c_v[b].rearrange("p t (k d) -> p t k d", d=D)).then_inc(cx_in, 16)

            def maxima_rows(b, par, hf):
                sp.wait_ge(x_free, fill_m(b, hf))
                hs = hf * NH // 2
                for part in range(2):
                    sp.dma_start(qs[96 + part:97 + part, par, hs:hs + NH // 2, :],
                                 mrow[16 * part:16 * part + 16, hf, :]).then_inc(mrow_in[hf], 16)

            def load_r(b):
                if not is_first(b):
                    sp.wait_ge(x2_ready, b)
                sp.dma_start(xr[:], x_v[b]).then_inc(xr_in, 16)

            def store(b):
                sp.wait_ge(x2_ready, b + 1)
                sp.dma_start(o_v[b], x2[:]).then_inc(x2_out, 16)
                sp.wait_ge(xs_ready, b + 1)
                sp.dma_start(pairs_v[b], xs[:].rearrange("p t a h -> p t (a h)")).then_inc(pairs_out, 16)

            def step(b, par):
                if has_a(b):
                    load_a(b + 2)
                maxima_rows(b, par, 1)
                if has_r(b):
                    store(b - 1)
                load_r(b)
                if has_p(b):
                    maxima_rows(b + 1, 1 - par, 0)

            load_a(1)
            maxima_rows(0, 0, 0)
            loops(sp, step)

            def weights(e, i):
                r = i % WRING
                n = CHUNKS * e + i
                if not (isinstance(n, int) and n < WRING):
                    sp.wait_ge(wpair_lo, n - WRING + 1)
                if i < FB:
                    for h in range(2):
                        sp.dma_start(wraw[:, r, :].rearrange("p (k h f) -> p k h f", k=KB, h=2)[:, :, h, :],
                                     gu_v[e][:, :, h, i * P:(i + 1) * P]).then_inc(w_in[r], 16)
                else:
                    for h in range(2):
                        sp.dma_start(wraw[:, r, h * 1024:(h + 1) * 1024].rearrange("p (k f) -> p k f", k=FB // 2),
                                     dn_v[e][:, 2 * h:2 * h + 2, (i - FB) * 512:(i - FB + 1) * 512]).then_inc(w_in[r], 16)

            def get_slots(e, par):
                if not (isinstance(e, int) and e < 2):
                    sp.wait_ge(added, 16 * CT * (e - 1))
                sp.dma_start(slots[:, par], lists_v[e]).then_inc(slots_in[par], 16)

            sp.wait_ge(x_full, of_p(nb - 1, "Q7"))
            for i in range(WRING):
                weights(0, i)
            store(nb - 1)
            sp.wait_ge(lists_out, 16 * T2 * TOPK * nb)
            sp.wait_ge(stage1, 4)
            sp.wait_ge(x2_out, 16 * nb)
            sp.wait_ge(pairs_out, 16 * nb)
            get_slots(0, 0)

            def step2(e, par, last):
                if not last:
                    get_slots(e + 1, 1 - par)
                for i in range(WRING, CHUNKS):
                    weights(e, i)
                if not last:
                    for i in range(WRING):
                        weights(e + 1, i)

            loops2(sp, step2)
            sp.wait_ge(added, 16 * CT * ne)

        @block.gpsimd
        def _(pool):
            def const(ins):
                ins.then_inc(pool_order, 1)
                pool_n[0] += 1
                pool.wait_ge(pool_order, pool_n[0])
            pool_n = [0]
            const(pool.iota(empty[:], pattern=[[0, NROUTED * CT], [0, 2]], base=int(NO_SLOT), channel_multiplier=0))
            pool.memset(ident[:], 0.0).then_inc(consts, 1)
            pool.wait_ge(consts, 1)
            const(pool.affine_select(out=ident[:], in_=ident[:], compare_op=ALU.not_equal, fill=1.0, base=0,
                                     pattern=[[-1, P]], channel_multiplier=1))
            const(pool.memset(ones[:], 1.0))
            const(pool.affine_select(out=tri[:], in_=ones[:], compare_op=ALU.is_gt, fill=0.0, base=0,
                                     pattern=[[1, P]], channel_multiplier=-1))
            const(pool.iota(iota_e[:], pattern=[[1, NROUTED]], base=0, channel_multiplier=0,
                            allow_small_or_imprecise_dtypes=True))
            const(pool.iota(slot0[:], pattern=[[CAP, NROUTED]], base=-int(NO_SLOT), channel_multiplier=0,
                            allow_small_or_imprecise_dtypes=True))
            const(pool.iota(token[:], pattern=[[P, T2], [0, TOPK]], base=0, channel_multiplier=1,
                            allow_small_or_imprecise_dtypes=True))
            const(pool.memset(half[:], -0.5))
            const(pool.memset(spare[:, 3:4], 0.0))
            const(pool.memset(pbias[:], P_LOG * 0.6931471805599453))
            const(pool.memset(carry[:], 0.0))
            const(pool.memset(kd[:], 1.0))
            const(pool.memset(ks[96:98, :, :, :], M_SCALE))
            pool.memset(half[:], -0.5).then_inc(consts, 1)
            pool.wait_ge(consts, 2)
            n0 = pool_n[0]

            def carry_wait(n):
                pool.wait_ge(pool_order, n0 + n)
                pool.tensor_tensor(spare[:, 2:3], spare[:, 3:4], spare[:, 3:4], ALU.mult).then_inc(pool_order, 1)

            def power(which, n):
                pool.wait_ge(var_ready, n)
                pool.tensor_tensor(rstd[:, which], veps[:, which], half[:], ALU.pow).then_inc(rstd_ready, 1)

            def norm1(b):
                power(0, nth_norm1(b))

            def norm2(b):
                power(1, nth_norm2(b))

            def low_q(b, par):
                if not (isinstance(b, int) and b < 2):
                    pool.wait_ge(x_full, of_p(b - 2, "Q7"))
                for t in range(T2):
                    pool.wait_ge(qhi_ready, 4 * b + 2 * t + 2)
                    pool.wait_ge(xn_ready, nth_norm1(b))
                    pool.tensor_tensor(qd[:, par, t, :, 2, :], xn[:, t].rearrange("p (h d) -> p h d", d=D),
                                       qd[:, par, t, :, 0, :], ALU.subtract).then_inc(qlo_ready, 1)

            def low_probs(b, kv):
                for tt in range(2):
                    if tt == 0 and kv % 2 == 0:
                        continue
                    u = 2 * kv + tt
                    pool.wait_ge(phi_dve if tt == 0 else phi_act, 8 * b + kv + 1)
                    if not (is_first(b) and kv < 4):
                        pool.wait_ge(v_full, 8 * b + kv - 3)
                    pool.tensor_tensor(plo[:, u % 8], prob[:, u % 4], phi[:, u % 8], ALU.subtract).then_inc(plo_pool, 1)

            def scatter(b, n0, n1):
                if n0 == 0:
                    pool.wait_ge(entry_ready, b + 1)
                    carry_wait(b)
                for n in range(n0, n1):
                    pool.indirect_dma_start(
                        out=lists, out_offset=bass.IndirectOffsetOnAxis(ap=dest[:, n:n + 1].bitcast(U32), axis=0),
                        in_=entry[:, n, :], in_offset=None, bounds_check=NROUTED * CAP - 1,
                        oob_is_err=False).then_inc(lists_out, 16)

            def step(b, par):
                for kv in range(KV):
                    if kv == 1 and has_r(b):
                        norm2(b - 1)
                    if kv == 3 and has_a(b):
                        norm1(b + 2)
                    low_probs(b, kv)
                    if kv == 4 and has_a(b):
                        low_q(b + 2, par)
                    if not (isinstance(b, int) and b < 2):
                        scatter(b - 2, 2 * kv, 2 * kv + 2)

            norm1(0)
            low_q(0, 0)
            norm1(1)
            low_q(1, 1)
            pool.wait_ge(lists_set, 16)
            loops(pool, step)
            norm2(nb - 1)
            for b in (nb - 2, nb - 1):
                scatter(b, 0, T2 * TOPK)
            pool.wait_ge(lists_out, 16 * T2 * TOPK * nb)
            pool.memset(slots[:], 0).then_inc(stage1, 1)
            pool.wait_ge(stage1, 4)
            pool.wait_ge(pairs_out, 16 * nb)
            pool.wait_ge(x2_out, 16 * nb)
            pool.memset(xg[:], 0.0).then_inc(pool_order, 1)
            n0 += nb + 1
            pool.wait_ge(pool_order, n0)

            def gather(e, par):
                pool.wait_ge(slots_in[par], 8 * e + 16 if par == 0 else 8 * (e + 1))
                if not is_first(e):
                    pool.wait_ge(gt_full, 8 * e)
                carry_wait(0 if is_first(e) else (CT + 1) * (e - 1) + 1)
                for c in range(CT):
                    pool.indirect_dma_start(
                        out=xg[:, c].rearrange("p a h -> p (a h)"), out_offset=None, in_=pairs,
                        in_offset=bass.IndirectOffsetOnAxis(ap=slots[:, par, c, 0:1].bitcast(U32), axis=0),
                        bounds_check=ntok - 1, oob_is_err=False).then_inc(gathered, 16)

            def add(e, par, last):
                if not is_first(e):
                    pool.wait_ge(added, 16 * CT * e)
                for c in range(CT):
                    pool.wait_ge(y_free, 8 * e + 5 + c)
                    carry_wait((CT + 1) * e + c + (2 if not last else 1))
                    pool.indirect_dma_start(
                        out=o_rows, out_offset=bass.IndirectOffsetOnAxis(ap=slots[:, par, c, 0:1].bitcast(U32), axis=0),
                        in_=ys[:, c, :], in_offset=None, bounds_check=ntok - 1, oob_is_err=False,
                        compute_op=ALU.add).then_inc(added, 16)

            def step2(e, par, last):
                if not last:
                    gather(e + 1, 1 - par)
                add(e, par, last)

            gather(0, 0)
            loops2(pool, step2)
            pool.wait_ge(added, 16 * CT * ne)

        @block.scalar
        def _(act):
            act.wait_ge(small_in, 64)
            act.activation(tgate[:], gates[:], ACT.Tanh).then_inc(setup_act, 1)
            act.activation(wcpair[:, 0, :], wcraw, ACT.Copy, scale=W_SCALE).then_inc(setup_act, 1)
            act.wait_ge(consts, 2)

            def hi_q(b, par):
                act.wait_ge(nmr_ready, nth_norm1(b))
                if not (isinstance(b, int) and b < 2):
                    act.wait_ge(x_full, of_p(b - 2, "Q7"))
                for t in range(T2):
                    for c in range(2):
                        act.activation(qd[:, par, t, :, c, :], x1[:, t].rearrange("p (h d) -> p h d", d=D), ACT.Identity,
                                       scale=rstd[:, 0, t:t + 1], bias=nmr[:, 0, t:t + 1]).then_inc(qhi_ready, 1)

            def hi_k(b):
                act.wait_ge(cx_in, 16 * (b + 1))
                if not is_first(b):
                    act.wait_ge(x_full, of_p(b - 1, "K1"))
                    act.wait_ge(vd_ready, b)
                for c in (0, 2):
                    act.activation(kd[:, :, :, c * D:(c + 1) * D], cx[:], ACT.Copy, scale=C_SCALE).then_inc(khi_ready, 1)

            def hi_x(b):
                act.wait_ge(nmr_ready, nth_norm2(b))
                if not is_first(b):
                    act.wait_ge(x_full, of_r(b - 1, "X3"))
                    act.wait_ge(pairs_out, 16 * b)
                for t in range(T2):
                    act.activation(xs[:, t, 0, :], x2[:, t], ACT.Identity, scale=rstd[:, 1, t:t + 1],
                                   bias=nmr[:, 1, t:t + 1]).then_inc(xhi_ready, 1)

            def k_stack(b, par):
                for u in range(2):
                    act.wait_ge(x_full, of_p(b, f"K{u}"))
                    act.activation(ks[0:96, par, 4 * u:4 * u + 4, :].rearrange("p k s -> p (k s)"), ps_x16[0:96, :],
                                   ACT.Copy).then_inc(x_free, 1)

            def q_stack(b, par, kv):
                act.wait_ge(x_full, of_p(b, f"Q{kv}"))
                act.activation(qs[0:96, par, G * kv:G * kv + G, :].rearrange("p k s -> p (k s)"), ps_x16[0:96, :],
                               ACT.Copy).then_inc(x_free, 1)

            def m_rows(b, hf):
                act.wait_ge(x_full, fill_m(b, hf))
                if not is_first(b):
                    act.wait_ge(mrow_in[hf], 32 * b)
                act.activation(mrow[:, hf, :], ps_x16[0:32, 0:S], ACT.Copy).then_inc(x_free, 1)

            def x_stack(b):
                for u in range(4):
                    t, part = u // 2, u % 2
                    act.wait_ge(x_full, of_r(b, f"X{u}"))
                    act.activation(xt[:, part, t].rearrange("p k s -> p (k s)"), ps_x16[:, :],
                                   ACT.Copy).then_inc(x_free, 1)

            def router_exp(b):
                act.wait_ge(lneg_ready, b + 1)
                for t in range(T2):
                    act.activation(lexp[:, t], lg[:, t], ACT.Exp, bias=lneg[:, t:t + 1],
                                   scale=1.0 / (XS_SCALE * W_SCALE)).then_inc(lexp_ready, 1)

            def low_done(b, kv, tt):
                if tt == 0 and kv % 2 == 0:
                    return plo_dve, 4 * b + kv // 2 + 1
                return plo_pool, 12 * b + 3 * (kv // 2) + (1 if kv % 2 == 0 else 2 + tt)

            def exps(b, kv):
                for tt in range(2):
                    u = 2 * kv + tt
                    act.wait_ge(t_full, 16 * b + u + 1)
                    if not (is_first(b) and kv < 2):
                        act.wait_ge(*(low_done(b, kv - 2, tt) if kv >= 2 else low_done(b - 1, kv + KV - 2, tt)))
                    act.activation(prob[:, u % 4], ps_t[:, tt], ACT.Exp, bias=pbias[:],
                                   scale=1.0 / (XS_SCALE * C_SCALE * float(D) ** 0.5)).then_inc(t_free, 1)

            def high_probs(b, kv):
                u = 2 * kv + 1
                act.wait_ge(t_free, 16 * b + u + 1)
                if not (is_first(b) and kv < 4):
                    act.wait_ge(v_full, 8 * b + kv - 3)
                act.activation(phi[:, u % 8], prob[:, u % 4], ACT.Copy).then_inc(phi_act, 1)

            def step(b, par):
                for kv in range(KV):
                    exps(b, kv)
                    if kv == 0 and has_p(b):
                        k_stack(b + 1, 1 - par)
                    if kv == 1:
                        m_rows(b, 1)
                    if kv == 3 and has_r(b):
                        x_stack(b - 1)
                    if kv == 4 and has_p(b):
                        m_rows(b + 1, 0)
                    if has_p(b):
                        q_stack(b + 1, 1 - par, kv)
                    high_probs(b, kv)
                    if kv == 2 and has_r(b):
                        hi_x(b - 1)
                    if kv == 4 and has_a(b):
                        hi_q(b + 2, par)
                        hi_k(b + 2)
                    if kv == 5 and has_r(b):
                        router_exp(b - 1)

            hi_q(0, 0)
            hi_k(0)
            k_stack(0, 0)
            for kv in range(KV):
                if kv == 4:
                    m_rows(0, 0)
                q_stack(0, 0, kv)
            hi_q(1, 1)
            hi_k(1)
            loops(act, step)
            hi_x(nb - 1)
            x_stack(nb - 1)
            router_exp(nb - 1)
            act.wait_ge(lexp_ready, 2 * nb)
            act.activation(tgate[:, 0:1], pbias[:], ACT.Copy).then_inc(stage1, 1)
            act.wait_ge(stage1, 4)

            def split_hi(e, i):
                n = CHUNKS * e + i
                r = i % WRING
                act.wait_ge(w_in[r], 32 * (2 * e + i // WRING + 1))
                if i >= WRING:
                    act.wait_ge(gu_full, 2 * (FB * e + i - WRING + 1))
                elif not is_first(e):
                    if i == 0:
                        act.wait_ge(gu_full, 2 * FB * e)
                    else:
                        act.wait_ge(y_full, 8 * e - 8 + 4 * i)
                act.activation(wpair[:, r, 0], wraw[:, r], ACT.Copy, scale=W_SCALE).then_inc(wpair_hi, 1)

            def silu(e, j):
                n = FB * e + j
                act.wait_ge(gu_full, 2 * n + 1)
                if not (isinstance(n, int) and n < 2):
                    act.wait_ge(a32_ready, n - 1)
                act.activation(sg[:, j % 2], ps_gu[:, j % 2, 0], ACT.Silu, scale=1.0 / (XS_SCALE * W_SCALE)).then_inc(sg_ready, 1)

            def act_hi(e, j):
                n = FB * e + j
                act.wait_ge(a32_ready, n + 1)
                if not is_first(e) and j == 0:
                    act.wait_ge(y_full, 8 * e)
                act.activation(apair[:, 0, j], a32[:, j % 2], ACT.Copy).then_inc(ahi_ready, 1)

            def y_out(e, par, m):
                n, c = m // CT, m % CT
                act.wait_ge(y_full, 8 * e + m + 1)
                if not is_first(e) and n == 0 and c == 0:
                    act.wait_ge(added, 16 * CT * e)
                act.activation(ys[:, c, n * 512:(n + 1) * 512], ps_y[:, m % 2], ACT.Copy,
                               scale=slots[:, par, c, 1:2].bitcast(F32)).then_inc(y_free, 1)

            def step2(e, par, last):
                act.wait_ge(slots_in[par], 8 * e + 16 if par == 0 else 8 * (e + 1))
                for j in range(FB):
                    if j + 2 < CHUNKS:
                        split_hi(e, j + 2)
                    silu(e, j)
                    act_hi(e, j)
                for m in range(8):
                    if m == 0 and not last:
                        split_hi(e + 1, 0)
                    if m == 4 and not last:
                        split_hi(e + 1, 1)
                    y_out(e, par, m)

            split_hi(0, 0)
            split_hi(0, 1)
            loops2(act, step2)

        @block.vector
        def _(dve):
            setup = Tally(dve, dve_order)

            def link(ins, tally):
                tally.add(ins)
                tally.wait()

            dve.wait_ge(setup_act, 2)
            dve.tensor_scalar(tg_at[:], tgate[:, 0:1], 1.0 / C_SCALE, None, ALU.mult).then_inc(setup_dve, 1)
            dve.tensor_scalar(tg_ff[:], tgate[:, 1:2], ROUTE_SCALE / (A_SCALE * W_SCALE), None, ALU.mult).then_inc(setup_dve, 1)
            dve.scalar_tensor_tensor(out=wcpair[:, 1, :], in0=wcraw, scalar=W_SCALE, in1=wcpair[:, 0, :],
                                     op0=ALU.mult, op1=ALU.subtract).then_inc(setup_dve, 1)
            for u in range(2):
                dve.wait_ge(wc_t, u + 1)
                dve.tensor_copy(wc[:, :, u, :], ps_x16[:, 0:KB * NALL].rearrange("p (k e) -> p k e", k=KB)).then_inc(setup_dve, 1)
            dve.wait_ge(consts, 2)
            dve.wait_ge(setup_dve, 5)

            def carry_wait(tally):
                tally.add(dve.memset(spare[:, 0:1], 0.0))

            def norm_stats(src, which, tally):
                for t in range(T2):
                    for c in range(2):
                        tally.add(dve.bn_stats(stats[:, which, t, c], src[:, t, 512 * c:512 * c + 512]))
                tally.wait()
                carry_wait(tally)
                for t in range(T2):
                    tally.add(dve.bn_aggr(mv[:, which, t], stats[:, which, t]))
                tally.wait()
                scale = XS_SCALE ** -2
                dve.tensor_scalar(veps[:, which], mv[:, which, :, 1], scale, LN_EPS * scale, ALU.mult, ALU.add).then_inc(var_ready, 1)

            def norm_apply(src, which, n, tally):
                dve.wait_ge(rstd_ready, n)
                dve.scalar_tensor_tensor(out=nmr[:, which], in0=mv[:, which, :, 0], scalar=-1.0, in1=rstd[:, which],
                                         op0=ALU.mult, op1=ALU.mult).then_inc(nmr_ready, 1)
                dve.wait_ge(nmr_ready, n)
                for t in range(T2):
                    ins = dve.tensor_scalar(xn[:, t], src[:, t], rstd[:, which, t:t + 1], nmr[:, which, t:t + 1],
                                            ALU.mult, ALU.add)
                    if t == 0:
                        tally.add(ins)
                ins.then_inc(xn_ready, 1)

            def stats_q(b, tally):
                dve.wait_ge(x1_in, 16 * (b + 1))
                norm_stats(x1, 0, tally)

            def apply_q(b, tally):
                if not is_first(b):
                    dve.wait_ge(qlo_ready, 2 * b)
                norm_apply(x1, 0, nth_norm1(b), tally)

            def low_k(b):
                dve.wait_ge(khi_ready, 2 * b + 2)
                dve.scalar_tensor_tensor(out=kd[:, :, :, D:2 * D].rearrange("p t k d -> p (t k) d"),
                                         in0=cx[:].rearrange("p t k d -> p (t k) d"), scalar=C_SCALE,
                                         in1=kd[:, :, :, 0:D].rearrange("p t k d -> p (t k) d"),
                                         op0=ALU.mult, op1=ALU.subtract).then_inc(kd_ready, 1)

            def keep_k(b, par):
                dve.wait_ge(kd_ready, b + 1)
                if not (isinstance(b, int) and b < 2):
                    dve.wait_ge(v_full, 8 * (b - 1))
                dve.tensor_copy(vd[:, par].rearrange("p t k d -> p (t k d)"), kd[:].rearrange("p t k d -> p (t k d)")).then_inc(vd_ready, 1)

            def maxima(b, kv):
                for t in range(T2):
                    for pr in range(2):
                        n = 32 * b + 4 * kv + 2 * t + pr
                        dve.wait_ge(s_full, n + 1)
                        if kv % 4 == 0 and t == 0 and pr == 0 and not is_first(b):
                            dve.wait_ge(mpair_ready, 2 * b + kv // 4 - 1)
                        h = G * kv + 2 * pr
                        dve.tensor_reduce(mx[:, t, h:h + 2], ps_s[:, pr].rearrange("p (h s) -> p h s", h=2),
                                          AXX, ALU.max).then_inc(s_free, 1)

            def max_pairs(b, hf, tally):
                dve.wait_ge(s_free, 32 * b + 16 * (hf + 1))
                if not is_first(b):
                    dve.wait_ge(x_full, fill_m(b - 1, hf))
                src = mx[:, :, hf * 16:hf * 16 + 16]
                link(dve.tensor_scalar(mpair[:, hf, :, 0, :], src, -1.0 / M_SCALE, None, ALU.mult), tally)
                dve.scalar_tensor_tensor(out=mpair[:, hf, :, 1, :], in0=src, scalar=-1.0 / M_SCALE,
                                         in1=mpair[:, hf, :, 0, :], op0=ALU.mult, op1=ALU.subtract).then_inc(mpair_ready, 1)

            def high_probs(b, kv):
                u = 2 * kv
                dve.wait_ge(t_free, 16 * b + u + 1)
                if not (is_first(b) and kv < 4):
                    dve.wait_ge(v_full, 8 * b + kv - 3)
                dve.tensor_copy(phi[:, u % 8], prob[:, u % 4]).then_inc(phi_dve, 1)

            def low_probs(b, kv):
                u = 2 * kv
                dve.wait_ge(phi_dve, 8 * b + kv + 1)
                dve.tensor_tensor(plo[:, u % 8], prob[:, u % 4], phi[:, u % 8], ALU.subtract).then_inc(plo_dve, 1)

            def heads_out(b, kv, tally):
                dve.wait_ge(v_full, 8 * b + kv + 1)
                link(dve.reciprocal(recip[:], ps_v[:, :, :, D]), tally)
                dve.tensor_tensor(at[:, :, G * kv:G * kv + G, :], ps_v[:, :, :, 0:D],
                                  recip[:].unsqueeze(3).to_broadcast([P, T2, G, D]), ALU.mult).then_inc(v_free, 1)

            def residual(b, tally):
                dve.wait_ge(xr_in, 16 * (b + 1))
                dve.wait_ge(v_free, 8 * (b + 1))
                if not is_first(b):
                    dve.wait_ge(x2_out, 16 * b)
                    dve.wait_ge(xs_ready, b)
                dve.scalar_tensor_tensor(out=x2[:].rearrange("p t h -> p (t h)"), in0=at[:].rearrange("p t h d -> p (t h d)"),
                                         scalar=tg_at[:], in1=xr[:].rearrange("p t h -> p (t h)"),
                                         op0=ALU.mult, op1=ALU.add).then_inc(x2_ready, 1)
                dve.wait_ge(x2_ready, b + 1)
                norm_stats(x2, 1, tally)

            def low_x(b, tally):
                dve.wait_ge(qlo_ready, 2 * min(b + 3, nb) if isinstance(b, int) else 2 * (b + 3))
                norm_apply(x2, 1, nth_norm2(b), tally)
                dve.wait_ge(xn_ready, nth_norm2(b))
                for t in range(T2):
                    dve.wait_ge(xhi_ready, 2 * b + t + 1)
                    ins = dve.tensor_tensor(xs[:, t, 1], xn[:, t], xs[:, t, 0], ALU.subtract)
                    if t == 0:
                        tally.add(ins)
                ins.then_inc(xs_ready, 1)

            def bc(ap, shape):
                return ap.to_broadcast(shape)

            def router_a(b, tally):
                dve.wait_ge(x_full, of_r(b, "L"))
                dve.tensor_reduce(lg[:], ps_x[:, 0:2 * T2 * NALL].rearrange("p (t a e) -> p t e a", t=T2, a=2),
                                  AXX, ALU.add).then_inc(x_free, 1)
                dve.wait_ge(x_free, of_r(b, "L"))
                link(dve.tensor_reduce(lmax[:], lg[:], AXX, ALU.max), tally)
                dve.tensor_scalar(lneg[:], lmax[:], -1.0 / (XS_SCALE * W_SCALE), None, ALU.mult).then_inc(lneg_ready, 1)

            def router_b(b, tally):
                dve.wait_ge(lexp_ready, 2 * b + 2)
                link(dve.tensor_reduce(lsum[:], lexp[:], AXX, ALU.add), tally)
                link(dve.reciprocal(lrec[:], lsum[:]), tally)
                link(dve.tensor_tensor(score[:], lexp[:], bc(lrec[:].unsqueeze(2), [P, T2, NALL]), ALU.mult), tally)
                link(dve.tensor_tensor(biased[:], score[:], bc(bias_b[:].unsqueeze(1), [P, T2, NALL]), ALU.add), tally)
                carry_wait(tally)
                for t in range(T2):
                    tally.add(dve.max(top[:, t], biased[:, t]))
                tally.wait()
                carry_wait(tally)
                for t in range(T2):
                    tally.add(dve.max_index(topi[:, t], top[:, t], biased[:, t]))
                    tally.add(dve.match_replace(left[:, t], top[:, t], biased[:, t], -1e30))
                tally.wait()
                dve.tensor_tensor(mask[:], left[:], biased[:], ALU.not_equal).then_inc(mask_ready, 1)
                tally.add(dve.tensor_copy(topf[:], topi[:]))
                dve.wait_ge(mask_ready, b + 1)
                link(dve.tensor_tensor(wsel[:], score[:], mask[:], ALU.mult), tally)
                tally.add(dve.tensor_reduce(wsum[:, :, 0], wsel[:], AXX, ALU.add))
                tally.add(dve.tensor_reduce(wzero[:, :, 0], wsel[:, :, NROUTED:], AXX, ALU.add))
                tally.add(dve.tensor_tensor(hot[:].rearrange("p t k e -> p (t k) e"),
                                            bc(iota_e[:].unsqueeze(1), [P, T2 * TOPK, NROUTED]),
                                            bc(topf[:].rearrange("p t k -> p (t k)").unsqueeze(2), [P, T2 * TOPK, NROUTED]),
                                            ALU.is_equal))
                tally.wait()
                link(dve.tensor_scalar(wsum[:], wsum[:], ROUTE_EPS, None, ALU.add), tally)
                link(dve.reciprocal(wrec[:], wsum[:]), tally)
                link(dve.tensor_tensor(wzero[:], wzero[:], wrec[:], ALU.mult), tally)
                link(dve.tensor_scalar(wzero[:], wzero[:], ROUTE_SCALE, 1.0, ALU.mult, ALU.add), tally)
                link(dve.scalar_tensor_tensor(out=wfac[:, :, 0], in0=wzero[:, :, 0], scalar=tg_ff[:], in1=wrec[:, :, 0],
                                              op0=ALU.mult, op1=ALU.mult), tally)
                link(dve.tensor_tensor(coef[:], wsel[:, :, 0:NROUTED], bc(wfac[:], [P, T2, NROUTED]), ALU.mult), tally)

            def router_c(b, tally):
                dve.wait_ge(x_full, of_r(b, "C"))
                px = ps_x[:, 0:3 * NROUTED].rearrange("p (t e) -> p t e", t=3)
                link(dve.tensor_tensor(pos[:], px[:, 0:2], bc(carry[:].unsqueeze(1), [P, T2, NROUTED]), ALU.add), tally)
                dve.tensor_tensor(carry[:], px[:, 2], carry[:], ALU.add).then_inc(x_free, 1)
                link(dve.tensor_tensor(place[:], pos[:], bc(slot0[:].unsqueeze(1), [P, T2, NROUTED]), ALU.add), tally)
                link(dve.scalar_tensor_tensor(out=place[:], in0=pos[:], scalar=float(CAP), in1=place[:],
                                              op0=ALU.is_lt, op1=ALU.mult), tally)
                for w, src in ((0, place), (1, coef)):
                    for t in range(T2):
                        tally.add(dve.tensor_tensor(pick[:, w, t], hot[:, t], bc(src[:, t].unsqueeze(1), [P, TOPK, NROUTED]), ALU.mult))
                tally.wait()
                link(dve.tensor_reduce(picked[:], pick[:].rearrange("p w t k e -> p w (t k) e"), AXX, ALU.add), tally)
                if not is_first(b):
                    dve.wait_ge(lists_out, 16 * T2 * TOPK * b)
                tally.add(dve.tensor_scalar(dest[:], picked[:, 0], NO_SLOT, None, ALU.add))
                tally.add(dve.tensor_copy(entry[:, :, 1].bitcast(F32), picked[:, 1]))
                link(dve.tensor_copy(entry[:, :, 0], token[:].rearrange("p t k -> p (t k)")), tally)
                dve.tensor_scalar(token[:], token[:], float(S), None, ALU.add).then_inc(entry_ready, 1)
                dve.wait_ge(entry_ready, b + 1)

            N_STATS, N_APPLY, N_RESIDUAL, N_LOW_X, N_PAIRS, N_OUT, N_RA, N_RB, N_RC = 7, 1, 7, 2, 1, 1, 1, 23, 11
            N_R = N_RESIDUAL + N_LOW_X + N_RA + N_RB + N_RC
            N_AHEAD = 2 * (N_STATS + N_APPLY) + N_PAIRS
            N_FIRST = N_STATS + N_APPLY + 2 * N_PAIRS + (KV - 1) * N_OUT
            N_FULL = N_STATS + N_APPLY + 2 * N_PAIRS + KV * N_OUT + N_R

            def orders(b):
                if is_first(b):
                    return N_AHEAD
                n = N_AHEAD + N_FIRST + N_FULL * (b - 1)
                if isinstance(b, int):
                    n -= max(0, b - (nb - 2)) * (N_STATS + N_APPLY) + max(0, b - (nb - 1)) * N_PAIRS
                return n

            def step(b, par):
                tally = Tally(dve, dve_order, orders(b))
                for kv in range(KV):
                    if kv == 0:
                        max_pairs(b, 1, tally)
                    if kv == 5 and has_r(b):
                        router_a(b - 1, tally)
                    high_probs(b, kv)
                    if kv % 2 == 0:
                        low_probs(b, kv)
                    if kv == 4 and has_p(b):
                        max_pairs(b + 1, 0, tally)
                    if kv == 7 and has_r(b):
                        router_c(b - 1, tally)
                    if kv == 1 and has_r(b):
                        residual(b - 1, tally)
                    if kv > 0:
                        heads_out(b, kv - 1, tally)
                    elif has_r(b):
                        heads_out(b - 1, KV - 1, tally)
                    if kv == 6 and has_r(b):
                        router_b(b - 1, tally)
                    if has_p(b):
                        maxima(b + 1, kv)
                    if kv == 2:
                        if has_r(b):
                            low_x(b - 1, tally)
                        if has_p(b):
                            keep_k(b + 1, 1 - par)
                    if kv == 3 and has_a(b):
                        stats_q(b + 2, tally)
                    if kv == 4 and has_a(b):
                        apply_q(b + 2, tally)
                        low_k(b + 2)
                tally.close(N_FULL - (0 if has_a(b) else N_STATS + N_APPLY) - (0 if has_p(b) else N_PAIRS)
                            - (0 if has_r(b) else N_R + N_OUT))

            tally = Tally(dve, dve_order, 0)
            stats_q(0, tally)
            apply_q(0, tally)
            low_k(0)
            for kv in range(KV):
                maxima(0, kv)
                if kv == 3:
                    max_pairs(0, 0, tally)
            keep_k(0, 0)
            stats_q(1, tally)
            apply_q(1, tally)
            low_k(1)
            tally.close(N_AHEAD)
            loops(dve, step)
            tally = Tally(dve, dve_order, orders(nb))
            heads_out(nb - 1, KV - 1, tally)
            residual(nb - 1, tally)
            low_x(nb - 1, tally)
            router_a(nb - 1, tally)
            router_b(nb - 1, tally)
            router_c(nb - 1, tally)
            dve.wait_ge(x_free, of_r(nb - 1, "C"))
            dve.tensor_copy(filled[:], carry[0:1, :]).then_inc(stage1, 1)
            dve.wait_ge(stage1, 4)

            def split_lo(e, i):
                n = CHUNKS * e + i
                r = i % WRING
                dve.wait_ge(wpair_hi, n + 1)
                dve.scalar_tensor_tensor(out=wpair[:, r, 1], in0=wraw[:, r], scalar=W_SCALE, in1=wpair[:, r, 0],
                                         op0=ALU.mult, op1=ALU.subtract).then_inc(wpair_lo, 1)

            def take_t(e, par, u):
                c, part = u // 2, u % 2
                dve.wait_ge(gt_full, 8 * e + u + 1)
                dve.tensor_copy(xgt[:, par, part, :, c * P:(c + 1) * P],
                                ps_g16[u % 2].rearrange("p (k t) -> p k t", k=KB)).then_inc(gt_free, 1)

            def gate_up(e, j):
                n = FB * e + j
                dve.wait_ge(gu_full, 2 * n + 2)
                dve.wait_ge(sg_ready, n + 1)
                if not (isinstance(n, int) and n < 2):
                    dve.wait_ge(alo_ready, n - 1)
                dve.scalar_tensor_tensor(out=a32[:, j % 2], in0=ps_gu[:, j % 2, 1],
                                         scalar=A_SCALE / (XS_SCALE * W_SCALE), in1=sg[:, j % 2],
                                         op0=ALU.mult, op1=ALU.mult).then_inc(a32_ready, 1)

            def act_lo(e, j):
                n = FB * e + j
                dve.wait_ge(ahi_ready, n + 1)
                dve.tensor_tensor(apair[:, 1, j], a32[:, j % 2], apair[:, 0, j], ALU.subtract).then_inc(alo_ready, 1)

            def step2(e, par, last):
                for j in range(FB):
                    if j + 2 < CHUNKS:
                        split_lo(e, j + 2)
                    gate_up(e, j)
                    act_lo(e, j)
                if not last:
                    for u in range(8):
                        take_t(e + 1, 1 - par, u)
                    split_lo(e + 1, 0)
                    split_lo(e + 1, 1)

            for u in range(8):
                take_t(0, 0, u)
            split_lo(0, 0)
            split_lo(0, 1)
            loops2(dve, step2)

        @block.tensor
        def _(pe):
            pe.wait_ge(consts, 2)
            pe.wait_ge(setup_act, 2)
            pe.wait_ge(setup_dve, 3)
            for u in range(2):
                if u:
                    pe.wait_ge(setup_dve, 4)
                for k in range(KB):
                    mm = pe.transpose(ps_x16[:, k * NALL:(k + 1) * NALL], wcpair[:, u, k * P:(k + 1) * P], ident[0:NALL, 0:NALL])
                mm.then_inc(wc_t, 1)
            pe.wait_ge(setup_dve, 5)

            def take_bank(n):
                if not (isinstance(n, int) and n == 1):
                    pe.wait_ge(x_free, n - 1)

            def k_transpose(b):
                pe.wait_ge(kd_ready, b + 1)
                for u in range(2):
                    take_bank(of_p(b, f"K{u}"))
                    for k in range(4):
                        for t in range(T2):
                            mm = pe.transpose(ps_x16[0:96, k * S + t * P:k * S + (t + 1) * P], kd[:, t, 4 * u + k, 0:96], ident[:])
                    mm.then_inc(x_full, 1)

            def q_transpose(b, par, kv):
                if kv == 0:
                    pe.wait_ge(qlo_ready, 2 * (b + 1))
                take_bank(of_p(b, f"Q{kv}"))
                for g in range(G):
                    for t in range(T2):
                        mm = pe.transpose(ps_x16[0:96, g * S + t * P:g * S + (t + 1) * P],
                                          qd[:, par, t, G * kv + g].rearrange("p c d -> p (c d)"), ident[:])
                mm.then_inc(x_full, 1)

            def m_transpose(b, hf):
                pe.wait_ge(mpair_ready, 2 * b + hf + 1)
                take_bank(fill_m(b, hf))
                for t in range(T2):
                    mm = pe.transpose(ps_x16[0:32, t * P:(t + 1) * P], mpair[:, hf, t].rearrange("p a h -> p (a h)"), ident[:])
                mm.then_inc(x_full, 1)

            def scores(b, par, kv):
                pe.wait_ge(x_free, of_p(b, f"Q{kv}"))
                for t in range(T2):
                    for pr in range(2):
                        n = 32 * b + 4 * kv + 2 * t + pr
                        if not (isinstance(n, int) and n < 2):
                            pe.wait_ge(s_free, n - 1)
                        for i in range(2):
                            h = G * kv + 2 * pr + i
                            mm = pe.matmul(ps_s[:, pr, i * S:(i + 1) * S], qs[0:96, par, h, t * P:(t + 1) * P],
                                           ks[0:96, par, kv, :], start=True, stop=True)
                        mm.then_inc(s_full, 1)

            def scores_t(b, par, kv):
                if kv % 4 == 0:
                    pe.wait_ge(mrow_in[kv // 4], 32 * (b + 1))
                for tt in range(2):
                    n = 16 * b + 2 * kv + tt
                    if not (isinstance(n, int) and n < 2):
                        pe.wait_ge(t_free, n - 1)
                    for pr in range(2):
                        h = G * kv + 2 * pr
                        mm = pe.matmul(ps_t[:, tt, 512 * pr:512 * pr + 512], ks[0:98, par, kv, tt * P:(tt + 1) * P],
                                       qs[0:98, par, h:h + 2, :], start=True, stop=True)
                    mm.then_inc(t_full, 1)

            def values(b, par, kv):
                if kv % 2 == 0:
                    pe.wait_ge(plo_dve, 4 * b + kv // 2 + 1)
                pe.wait_ge(plo_pool, 12 * b + 3 * (kv // 2) + (1 if kv % 2 == 0 else 3))
                if kv == 0:
                    pe.wait_ge(vd_ready, b + 1)
                n = 8 * b + kv
                if not (isinstance(n, int) and n == 0):
                    pe.wait_ge(v_free, n)
                for t in range(T2):
                    for g in range(G):
                        c0 = g * S + t * P
                        for tt in range(2):
                            r = (2 * kv + tt) % 8
                            pe.matmul(ps_v[:, t, g, :], phi[:, r, c0:c0 + P], vd[:, par, tt, kv, 64:97],
                                      start=(tt == 0), stop=False)
                            pe.matmul(ps_v[:, t, g, 0:D], phi[:, r, c0:c0 + P], vd[:, par, tt, kv, D:2 * D],
                                      start=False, stop=False)
                            mm = pe.matmul(ps_v[:, t, g, :], plo[:, r, c0:c0 + P], vd[:, par, tt, kv, 64:97],
                                           start=False, stop=(tt == 1))
                mm.then_inc(v_full, 1)

            def x_transpose(b, us):
                for u in us:
                    t, part = u // 2, u % 2
                    if u == 0:
                        pe.wait_ge(xs_ready, b + 1)
                    take_bank(of_r(b, f"X{u}"))
                    for k in range(KB):
                        mm = pe.transpose(ps_x16[:, k * P:(k + 1) * P], xs[:, t, part, k * P:(k + 1) * P], ident[:])
                    mm.then_inc(x_full, 1)

            def logits(b):
                pe.wait_ge(x_free, of_r(b, "X3"))
                take_bank(of_r(b, "L"))
                for t in range(T2):
                    for part in range(2):
                        for k in range(KB):
                            mm = pe.matmul(ps_x[:, t * 2 * NALL:(t + 1) * 2 * NALL], xt[:, part, t, k, :],
                                           wc[:, k].rearrange("p a e -> p (a e)"), start=(part == 0 and k == 0),
                                           stop=(part == 1 and k == KB - 1))
                mm.then_inc(x_full, 1)

            def counts(b):
                pe.wait_ge(mask_ready, b + 1)
                take_bank(of_r(b, "C"))
                m0, m1 = mask[:, 0, 0:NROUTED], mask[:, 1, 0:NROUTED]
                n = NROUTED
                pe.matmul(ps_x[:, 0:n], tri[:], m0, start=True, stop=True)
                pe.matmul(ps_x[:, n:2 * n], ones[:], m0, start=True, stop=False)
                pe.matmul(ps_x[:, n:2 * n], tri[:], m1, start=False, stop=True)
                pe.matmul(ps_x[:, 2 * n:3 * n], ones[:], m0, start=True, stop=False)
                pe.matmul(ps_x[:, 2 * n:3 * n], ones[:], m1, start=False, stop=True).then_inc(x_full, 1)

            def step(b, par):
                for kv in range(KV):
                    scores_t(b, par, kv)
                    if kv == 0 and has_p(b):
                        k_transpose(b + 1)
                    if kv == 1:
                        m_transpose(b, 1)
                    if kv == 3 and has_r(b):
                        x_transpose(b - 1, range(4))
                    if kv == 4 and has_p(b):
                        m_transpose(b + 1, 0)
                    if has_p(b):
                        q_transpose(b + 1, 1 - par, kv)
                    if kv > 0:
                        values(b, par, kv - 1)
                    elif has_r(b):
                        values(b - 1, 1 - par, KV - 1)
                    if has_p(b):
                        scores(b + 1, 1 - par, kv)
                    if kv == 4 and has_r(b):
                        logits(b - 1)
                    if kv == 6 and has_r(b):
                        counts(b - 1)

            k_transpose(0)
            for kv in range(KV):
                if kv == 4:
                    m_transpose(0, 0)
                q_transpose(0, 0, kv)
                scores(0, 0, kv)
            loops(pe, step)
            values(nb - 1, 1, KV - 1)
            x_transpose(nb - 1, range(4))
            logits(nb - 1)
            counts(nb - 1)
            pe.wait_ge(x_free, of_r(nb - 1, "C"))
            pe.transpose(ps_x16[0:32, 0:P], ident[:, 0:32], ident[:]).then_inc(stage1, 1)
            pe.wait_ge(stage1, 4)

            def t_rows(e, us):
                for u in us:
                    c, part = u // 2, u % 2
                    if u == 0:
                        pe.wait_ge(gathered, 16 * CT * (e + 1))
                    n = 8 * e + u
                    if not (isinstance(n, int) and n < 2):
                        pe.wait_ge(gt_free, n - 1)
                    for k in range(KB):
                        mm = pe.transpose(ps_g16[u % 2][:, k * P:(k + 1) * P], xg[:, c, part, k * P:(k + 1) * P], ident[:])
                    mm.then_inc(gt_full, 1)

            TERMS = ((0, 0), (0, 1), (1, 0))

            def up(e, par, j, nt):
                n = FB * e + j
                pe.wait_ge(wpair_lo, CHUNKS * e + j + 1)
                if not (isinstance(n, int) and n < 2):
                    pe.wait_ge(a32_ready, n - 1)
                w = wpair[:, j % WRING].rearrange("p a (k h f) -> p a k h f", k=KB, h=2)
                for h in range(2):
                    for k in range(KB):
                        for a, c in TERMS:
                            mm = pe.matmul(ps_gu[:, j % 2, h, 0:nt * P], w[:, a, k, h, :], xgt[:, par, c, k, 0:nt * P],
                                           start=(k == 0 and (a, c) == (0, 0)), stop=(k == KB - 1 and a == 1))
                    mm.then_inc(gu_full, 1)

            def down(e, n2, nt):
                i = FB + n2
                pe.wait_ge(wpair_lo, CHUNKS * e + i + 1)
                pe.wait_ge(alo_ready, FB * (e + 1))
                w = wpair[:, i % WRING].rearrange("p a (k h) -> p a k h", k=FB)
                for c in range(CT):
                    m = CT * n2 + c
                    n = 8 * e + m
                    if not (isinstance(n, int) and n < 2):
                        pe.wait_ge(y_free, n - 1)
                    if c >= nt:
                        pe.matmul(ps_y[:, m % 2, 0:2], ident[:], ident[:, 0:2], start=True, stop=True).then_inc(y_full, 1)
                        continue
                    for k in range(FB):
                        for a, o in ((0, 0), (1, 0), (0, 1)):
                            mm = pe.matmul(ps_y[:, m % 2], apair[:, o, k, c * P:(c + 1) * P], w[:, a, k, :],
                                           start=(k == 0 and (a, o) == (0, 0)), stop=(k == FB - 1 and o == 1))
                    mm.then_inc(y_full, 1)

            def products(e, par, last, nt):
                for j in range(FB):
                    up(e, par, j, nt)
                if not last:
                    t_rows(e + 1, range(8))
                for n2 in range(2):
                    down(e, n2, nt)

            def step2(e, par, last):
                if is_first(e):
                    products(e, par, last, CT)
                    return
                n = pe.value_load(filled[0:1, bass.ds(e, 1)], min_val=0, max_val=ntok)
                with pe.If(n < 2 * P + 1):
                    with pe.If(n < P + 1):
                        products(e, par, last, 1)
                    with pe.Else():
                        products(e, par, last, 2)
                with pe.Else():
                    with pe.If(n < 3 * P + 1):
                        products(e, par, last, 3)
                    with pe.Else():
                        products(e, par, last, 4)

            t_rows(0, range(8))
            pe.wait_ge(gt_free, 8)
            loops2(pe, step2)


_INS = ['x', 'ctx_512', 'g_xattn', 'g_ffn', 'L0_ffn_w_cls', 'L0_ffn_bias', 'L0_ffn_w_gate_up', 'L0_ffn_w_down']
_OUTS = [((16, 256, 1024), 'float32')]


def kernel(**inputs):
    import numpy as _np
    import concourse.bacc as _bacc
    from concourse import mybir as _mybir
    from concourse.bass_utils import run_bass_kernel_spmd as _run

    nc = _bacc.Bacc("TRN2", target_bir_lowering=False, num_devices=1)
    arrays, args = {}, []
    for name in _INS:
        a = _np.ascontiguousarray(inputs[name])
        arrays[f"in_{name}_dram"] = a
        args.append(nc.dram_tensor(f"in_{name}_dram", a.shape, _mybir.dt.from_np(a.dtype), kind="ExternalInput").ap())
    for i, (shape, dtype) in enumerate(_OUTS):
        dt = _mybir.dt.from_np(_np.dtype(dtype))
        args.append(nc.dram_tensor(f"out_{i}_dram", shape, dt, kind="ExternalOutput").ap())
    gated_block_kernel(nc, *args)
    r = _run(nc, [arrays], core_ids=[0])
    return r.results[0]["out_0_dram"]
```

```python
from contextlib import ExitStack

import concourse.bass as bass
from concourse import mybir

F32 = mybir.dt.float32
F16 = mybir.dt.float16
I32 = mybir.dt.int32
U32 = mybir.dt.uint32
ALU = mybir.AluOpType
ACT = mybir.ActivationFunctionType
AXX = mybir.AxisListType.X

P = 128
D = 32
G = 4
KV = 8
NH = G * KV
S = 256
T2 = S // P
H = NH * D
KB = H // P
NROUTED = 32
NALL = 64
TOPK = 8
CAP = 512
CT = CAP // P
FF = 512
FB = FF // P
ROUTE_SCALE = 1.5
LN_EPS = 1e-5
ROUTE_EPS = 1e-20

XS_SCALE = 64.0
C_SCALE = 16.0
W_SCALE = 256.0
A_SCALE = 32.0
M_SCALE = 32768.0
P_LOG = 12
NO_SLOT = float(1 << 20)


FILLS = ["K0", "Q0", "X1", "Q1", "M1", "X2", "Q2", "X3", "K1", "Q3", "L", "Q4", "Q5", "M0", "Q6", "C", "Q7", "X0"]
CHUNKS = FB + 2
ROWS_AFTER = ((), (0, 1), (2, 3), (4, 5, 6, 7))
AHEAD = 4


class Tally:

    def __init__(self, engine, sem, base=0):
        self.engine, self.sem, self.base, self.n = engine, sem, base, 0

    def add(self, instruction):
        instruction.then_inc(self.sem, 1)
        self.n += 1
        return self.base + self.n

    def wait(self, value=None):
        self.engine.wait_ge(self.sem, self.base + self.n if value is None else value)

    def close(self, steps):
        assert self.n == steps, (self.n, steps)


def gated_block_kernel(nc, x, ctx_512, g_xattn, g_ffn, w_cls, bias, w_gate_up, w_down, out, nb=16, ne=NROUTED):
    ntok = nb * S
    x_v = x.rearrange("b (t p) h -> b p t h", p=P)
    c_v = ctx_512.rearrange("b (t p) h -> b p t h", p=P)
    o_v = out.rearrange("b (t p) h -> b p t h", p=P)
    o_rows = out.rearrange("b s h -> (b s) h")
    gu_v = w_gate_up.rearrange("e (k p) (h f) -> e p k h f", p=P, h=2)
    dn_v = w_down.rearrange("e (k p) h -> e p k h", p=P)
    pairs = nc.dram_tensor("pairs", [ntok, 2 * H], F16).ap()
    lists = nc.dram_tensor("lists", [NROUTED * CAP, 2], I32).ap()
    pairs_v = pairs.rearrange("(b t p) h -> b p t h", p=P, t=T2)
    lists_v = lists.rearrange("(e c p) w -> e p c w", p=P, c=CT)
    lists_all = lists.rearrange("(p a) w -> p (a w)", p=P)

    with ExitStack() as whole:
        stack = [whole]

        def sb(name, shape, dt=F32):
            return stack[-1].enter_context(nc.sbuf_tensor(name, shape, dt))

        def sem(name):
            return whole.enter_context(nc.semaphore(name))

        psum = whole.enter_context(nc.psum_tensor("psum", [P, 8, 512], F32))

        ident = sb("ident", [P, P], F16)
        spare = sb("spare", [P, 4])
        filled = sb("filled", [1, NROUTED], I32)

        first = ExitStack()
        stack.append(first)
        qd = sb("qd", [P, 2, T2, NH, 3, D], F16)
        x1 = sb("x1", [P, T2, H])
        qs = sb("qs", [98, 2, NH, S], F16)
        ks = sb("ks", [98, 2, KV, S], F16)
        prob = sb("prob", [P, 4, G * S])
        phi = sb("phi", [P, 8, G * S], F16)
        xr = sb("xr", [P, T2, H])
        xn = sb("xn", [P, T2, H])
        cx = sb("cx", [P, T2, KV, D])
        kd = sb("kd", [P, T2, KV, 98], F16)
        vd = sb("vd", [P, 2, T2, KV, 98], F16)
        mx = sb("mx", [P, T2, NH])
        mpair = sb("mpair", [P, 2, T2, 2, NH // 2], F16)
        mrow = sb("mrow", [32, 2, S], F16)
        plo = sb("plo", [P, 8, G * S], F16)
        at = sb("at", [P, T2, NH, D])
        x2 = sb("x2", [P, T2, H])
        xs = sb("xs", [P, T2, 2, H], F16)
        xt = sb("xt", [P, 2, T2, KB, P], F16)
        wc = sb("wc", [P, KB, 2, NALL], F16)
        stats = sb("stats", [P, 2, T2, 2, 6])
        mv = sb("mv", [P, 2, T2, 2])
        veps = sb("veps", [P, 2, T2])
        rstd = sb("rstd", [P, 2, T2])
        nmr = sb("nmr", [P, 2, T2])
        half = sb("half", [P, T2])
        pbias = sb("pbias", [P, 1])
        recip = sb("recip", [P, T2, G])
        gates = sb("gates", [P, 2])
        tgate = sb("tgate", [P, 2])
        tg_at = sb("tg_at", [P, 1])
        tg_ff = sb("tg_ff", [P, 1])
        bias_b = sb("bias_b", [P, NALL])
        tri = sb("tri", [P, P], F16)
        ones = sb("ones", [P, P], F16)
        iota_e = sb("iota_e", [P, NROUTED])
        slot0 = sb("slot0", [P, NROUTED])
        token = sb("token", [P, T2, TOPK])
        lg = sb("lg", [P, T2, NALL])
        lmax = sb("lmax", [P, T2])
        lneg = sb("lneg", [P, T2])
        lexp = sb("lexp", [P, T2, NALL])
        lsum = sb("lsum", [P, T2])
        lrec = sb("lrec", [P, T2])
        score = sb("score", [P, T2, NALL])
        biased = sb("biased", [P, T2, NALL])
        top = sb("top", [P, T2, TOPK])
        topi = sb("topi", [P, T2, TOPK], U32)
        topf = sb("topf", [P, T2, TOPK])
        left = sb("left", [P, T2, NALL])
        mask = sb("mask", [P, T2, NALL], F16)
        wsel = sb("wsel", [P, T2, NALL])
        wsum = sb("wsum", [P, T2, 1])
        wzero = sb("wzero", [P, T2, 1])
        wrec = sb("wrec", [P, T2, 1])
        wfac = sb("wfac", [P, T2, 1])
        coef = sb("coef", [P, T2, NROUTED])
        pos = sb("pos", [P, T2, NROUTED])
        place = sb("place", [P, T2, NROUTED])
        carry = sb("carry", [P, NROUTED])
        hot = sb("hot", [P, T2, TOPK, NROUTED])
        pick = sb("pick", [P, 2, T2, TOPK, NROUTED])
        picked = sb("picked", [P, 2, T2 * TOPK])
        dest = sb("dest", [P, T2 * TOPK], I32)
        entry = sb("entry", [P, T2 * TOPK, 2], I32)
        wcraw = at[0:NALL, 0].rearrange("p h d -> p (h d)")
        wcpair = phi[0:NALL, 0:2, :]
        empty = sb("empty", [P, NROUTED * CT, 2], I32)
        stack.pop()
        first.close()

        wraw = sb("wraw", [P, CHUNKS, 2048])
        wpair = sb("wpair", [P, CHUNKS, 2, 2048], F16)
        xg = sb("xg", [P, CT, 2, H], F16)
        xgt = sb("xgt", [P, 2, 2, KB, CAP], F16)
        gslots = sb("gslots", [P, 2, CT, 2], I32)
        slots = sb("slots", [P, 2, CT, 2], I32)
        sg = sb("sg", [P, 2, CAP])
        a32 = sb("a32", [P, 2, CAP])
        apair = sb("apair", [P, 2, FB, CAP], F16)
        ys = sb("ys", [P, CT, H])

        ps_s = psum[:, 0:2, :]
        ps_t = psum[:, 2:6, :].rearrange("p (r b) n -> p r (b n)", r=2)
        ps_v = psum[:, 6, 0:T2 * G * 33].rearrange("p (t g d) -> p t g d", t=T2, g=G)
        ps_x = psum[:, 7, :]
        ps_x16 = psum[:, 7, :].bitcast(F16)
        ps_gu = psum[:, 0:4, :].rearrange("p (r h) n -> p r h n", r=2)
        ps_y = psum[:, 4:6, :]
        ps_g16 = [psum[:, 6, :].bitcast(F16), psum[:, 7, :].bitcast(F16)]

        small_in = sem("small_in")
        x1_in, cx_in, xr_in = sem("x1_in"), sem("cx_in"), sem("xr_in")
        mrow_in = [sem("mrow_in0"), sem("mrow_in1")]
        x2_out, pairs_out = sem("x2_out"), sem("pairs_out")
        lists_set, lists_out = sem("lists_set"), sem("lists_out")
        w_in = [sem(f"w_in{i}") for i in range(CHUNKS)]
        slots_in = [sem("slots_in0"), sem("slots_in1")]
        gslots_in = [sem("gslots_in0"), sem("gslots_in1")]
        xg_clear = sem("xg_clear")
        gathered = sem("gathered")
        added = sem("added")
        consts = sem("consts")
        dve_order = sem("dve_order")
        pool_order = sem("pool_order")
        setup_dve = sem("setup_dve")
        setup_act = sem("setup_act")
        wc_t = sem("wc_t")
        var_ready = sem("var_ready")
        rstd_ready = sem("rstd_ready")
        nmr_ready = sem("nmr_ready")
        qhi_ready = sem("qhi_ready")
        xn_ready = sem("xn_ready")
        qlo_ready = sem("qlo_ready")
        vd_ready = sem("vd_ready")
        khi_ready = sem("khi_ready")
        kd_ready = sem("kd_ready")
        x_full, x_free = sem("x_full"), sem("x_free")
        s_full, s_free = sem("s_full"), sem("s_free")
        stack_ready = sem("stack_ready")
        mpair_ready = sem("mpair_ready")
        t_full, t_free = sem("t_full"), sem("t_free")
        phi_dve, phi_act = sem("phi_dve"), sem("phi_act")
        plo_dve, plo_pool = sem("plo_dve"), sem("plo_pool")
        v_full, v_free = sem("v_full"), sem("v_free")
        x2_ready = sem("x2_ready")
        xhi_ready = sem("xhi_ready")
        xs_ready = sem("xs_ready")
        lneg_ready, lexp_ready = sem("lneg_ready"), sem("lexp_ready")
        mask_ready = sem("mask_ready")
        entry_ready = sem("entry_ready")
        stage1 = sem("stage1")
        wpair_hi, wpair_lo = sem("wpair_hi"), sem("wpair_lo")
        gt_full, gt_free = sem("gt_full"), sem("gt_free")
        gu_full = sem("gu_full")
        sg_ready, a32_ready = sem("sg_ready"), sem("a32_ready")
        ahi_ready, alo_ready = sem("ahi_ready"), sem("alo_ready")
        y_full, y_free = sem("y_full"), sem("y_free")

        def on(b, lag):
            return not isinstance(b, int) or 0 <= b + lag < nb

        def at_step(b, n):
            return isinstance(b, int) and b == n

        def fills_of(step):
            lag = {"K": 1, "Q": 1, "M": 1, "X": -2, "L": -2, "C": -2}
            return [f for f in FILLS if on(step, {"M1": 0, "X0": -1}.get(f, lag[f[0]]))]

        def nth_fill(step, name):
            if isinstance(step, int):
                return sum(len(fills_of(i)) for i in range(-2, step)) + fills_of(step).index(name) + 1
            return nth_fill(2, name) + len(FILLS) * (step - 2)

        def of_p(b, name):
            return nth_fill(b - 1, name)

        def of_r(b, name):
            return nth_fill(b + 1 if name == "X0" else b + 2, name)

        def fill_m(b, hf):
            return nth_fill(b, "M1") if hf else of_p(b, "M0")

        def nth_norm1(b):
            return 2 * b - 2 + (max(0, 3 - b) if isinstance(b, int) else 0)

        def nth_norm2(b):
            return 2 * b + 5 - (max(0, b + 4 - nb) if isinstance(b, int) else 0)

        def loops(eng, step):
            for b in range(-2, 3):
                step(b, b % 2)
            with eng.Fori(0, (nb - 6) // 2) as i:
                step(2 * i + 3, 1)
                step(2 * i + 4, 0)
            for b in range(nb - 3, nb + 3):
                step(b, b % 2)

        def is_first(b):
            return isinstance(b, int) and b == 0

        def loops2(eng, step):
            step(0, 0, False)
            with eng.Fori(0, (ne - 4) // 2) as i:
                step(2 * i + 1, 1, False)
                step(2 * i + 2, 0, False)
            for e in range(ne - 3, ne):
                step(e, e % 2, e == ne - 1)

        block = whole.enter_context(nc.Block())

        @block.sync
        def _(sp):
            sp.dma_start(gates[:, 0:1], g_xattn.rearrange("(a b) -> a b", a=1).to_broadcast([P, 1])).then_inc(small_in, 16)
            sp.dma_start(gates[:, 1:2], g_ffn.rearrange("(a b) -> a b", a=1).to_broadcast([P, 1])).then_inc(small_in, 16)
            sp.dma_start(bias_b[:], bias.rearrange("(a b) -> a b", a=1).to_broadcast([P, NALL])).then_inc(small_in, 16)
            sp.dma_start(wcraw, w_cls).then_inc(small_in, 16)
            sp.wait_ge(consts, 1)
            sp.dma_start(lists_all, empty[:].rearrange("p a w -> p (a w)")).then_inc(lists_set, 16)

            def load_a(b):
                if not is_first(b):
                    sp.wait_ge(qlo_ready, 2 * b)
                    sp.wait_ge(kd_ready, b)
                sp.dma_start(x1[:], x_v[b]).then_inc(x1_in, 16)
                sp.dma_start(cx[:], c_v[b].rearrange("p t (k d) -> p t k d", d=D)).then_inc(cx_in, 16)

            def maxima_rows(b, par, hf):
                sp.wait_ge(x_free, fill_m(b, hf))
                hs = hf * NH // 2
                for part in range(2):
                    sp.dma_start(qs[96 + part:97 + part, par, hs:hs + NH // 2, :],
                                 mrow[16 * part:16 * part + 16, hf, :]).then_inc(mrow_in[hf], 16)

            def load_r(b):
                if not is_first(b):
                    sp.wait_ge(x2_ready, b)
                sp.dma_start(xr[:], x_v[b]).then_inc(xr_in, 16)

            def store_x2(b):
                sp.wait_ge(x2_ready, b + 1)
                sp.dma_start(o_v[b], x2[:]).then_inc(x2_out, 16)

            def store_pairs(b):
                sp.wait_ge(xs_ready, b + 1)
                sp.dma_start(pairs_v[b], xs[:].rearrange("p t a h -> p t (a h)")).then_inc(pairs_out, 16)

            def step(b, par):
                if on(b, 2):
                    load_a(b + 2)
                if on(b, 0):
                    maxima_rows(b, par, 1)
                if on(b, -1):
                    store_x2(b - 1)
                if on(b, 0):
                    load_r(b)
                if on(b, 1):
                    maxima_rows(b + 1, 1 - par, 0)
                if on(b, -1):
                    store_pairs(b - 1)
                if at_step(b, nb - 1):
                    sp.wait_ge(x_full, of_p(nb - 1, "Q7"))
                    for i in range(4):
                        weights(0, i)
                if at_step(b, nb):
                    sp.wait_ge(t_full, 16 * nb)
                    for i in range(4, CHUNKS):
                        weights(0, i)

            def weights(e, i):
                if not is_first(e):
                    sp.wait_ge(wpair_lo, CHUNKS * (e - 1) + i + 1)
                if i < FB:
                    for h in range(2):
                        sp.dma_start(wraw[:, i, :].rearrange("p (k h f) -> p k h f", k=KB, h=2)[:, :, h, :],
                                     gu_v[e][:, :, h, i * P:(i + 1) * P]).then_inc(w_in[i], 16)
                else:
                    for h in range(2):
                        sp.dma_start(wraw[:, i, h * 1024:(h + 1) * 1024].rearrange("p (k f) -> p k f", k=FB // 2),
                                     dn_v[e][:, 2 * h:2 * h + 2, (i - FB) * 512:(i - FB + 1) * 512]).then_inc(w_in[i], 16)

            def get_slots(e, par):
                if not (isinstance(e, int) and e < 2):
                    sp.wait_ge(added, 16 * CT * (e - 1))
                sp.dma_start(slots[:, par], lists_v[e]).then_inc(slots_in[par], 16)

            loops(sp, step)
            sp.wait_ge(lists_out, 16 * T2 * TOPK * nb)
            sp.wait_ge(stage1, 4)
            sp.wait_ge(x2_out, 16 * nb)
            sp.wait_ge(pairs_out, 16 * nb)

            def get_gslots(e, par):
                if not (isinstance(e, int) and e < 2):
                    sp.wait_ge(gathered, 16 * CT * (e - 1))
                sp.dma_start(gslots[:, par], lists_v[e]).then_inc(gslots_in[par], 16)

            get_gslots(0, 0)
            get_gslots(1, 1)
            get_slots(0, 0)

            def step2(e, par, last):
                if not isinstance(e, int) or e + 2 < ne:
                    get_gslots(e + 2, par)
                if not last:
                    get_slots(e + 1, 1 - par)
                    for i in range(CHUNKS):
                        weights(e + 1, i)

            loops2(sp, step2)
            sp.wait_ge(added, 16 * CT * ne)

        @block.gpsimd
        def _(pool):
            def const(ins):
                ins.then_inc(pool_order, 1)
                pool_n[0] += 1
                pool.wait_ge(pool_order, pool_n[0])
            pool_n = [0]
            const(pool.iota(empty[:], pattern=[[0, NROUTED * CT], [0, 2]], base=int(NO_SLOT), channel_multiplier=0))
            pool.memset(ident[:], 0.0).then_inc(consts, 1)
            pool.wait_ge(consts, 1)
            const(pool.affine_select(out=ident[:], in_=ident[:], compare_op=ALU.not_equal, fill=1.0, base=0,
                                     pattern=[[-1, P]], channel_multiplier=1))
            const(pool.memset(ones[:], 1.0))
            const(pool.affine_select(out=tri[:], in_=ones[:], compare_op=ALU.is_gt, fill=0.0, base=0,
                                     pattern=[[1, P]], channel_multiplier=-1))
            const(pool.iota(iota_e[:], pattern=[[1, NROUTED]], base=0, channel_multiplier=0,
                            allow_small_or_imprecise_dtypes=True))
            const(pool.iota(slot0[:], pattern=[[CAP, NROUTED]], base=-int(NO_SLOT), channel_multiplier=0,
                            allow_small_or_imprecise_dtypes=True))
            const(pool.iota(token[:], pattern=[[P, T2], [0, TOPK]], base=0, channel_multiplier=1,
                            allow_small_or_imprecise_dtypes=True))
            const(pool.memset(half[:], -0.5))
            const(pool.memset(spare[:, 3:4], 0.0))
            const(pool.memset(pbias[:], P_LOG * 0.6931471805599453))
            const(pool.memset(carry[:], 0.0))
            const(pool.memset(kd[:], 1.0))
            const(pool.memset(ks[96:98, :, :, :], M_SCALE))
            pool.memset(half[:], -0.5).then_inc(consts, 1)
            pool.wait_ge(consts, 2)
            n0 = pool_n[0]

            def carry_wait(n):
                pool.wait_ge(pool_order, n0 + n)
                pool.tensor_tensor(spare[:, 2:3], spare[:, 3:4], spare[:, 3:4], ALU.mult).then_inc(pool_order, 1)

            def power(which, n):
                pool.wait_ge(var_ready, n)
                pool.tensor_tensor(rstd[:, which], veps[:, which], half[:], ALU.pow).then_inc(rstd_ready, 1)

            def norm1(b):
                power(0, nth_norm1(b))

            def norm2(b):
                power(1, nth_norm2(b))

            def low_q(b, par, t):
                pool.wait_ge(qhi_ready, 4 * b + 2 * t + 2)
                pool.wait_ge(xn_ready, b + 1)
                pool.tensor_tensor(qd[:, par, t, :, 2, :], xn[:, t].rearrange("p (h d) -> p h d", d=D),
                                   qd[:, par, t, :, 0, :], ALU.subtract).then_inc(qlo_ready, 1)

            def low_probs(b, kv):
                for tt in range(2):
                    if tt == 0 and kv % 2 == 0:
                        continue
                    u = 2 * kv + tt
                    pool.wait_ge(phi_dve if tt == 0 else phi_act, 8 * b + kv + 1)
                    if not (is_first(b) and kv < 4):
                        pool.wait_ge(v_full, 8 * b + kv - 3)
                    pool.tensor_tensor(plo[:, u % 8], prob[:, u % 4], phi[:, u % 8], ALU.subtract).then_inc(plo_pool, 1)

            def scatter(b, n0, n1):
                if n0 == 0:
                    if is_first(b):
                        pool.wait_ge(lists_set, 16)
                    pool.wait_ge(entry_ready, b + 1)
                    carry_wait(b)
                for n in range(n0, min(n1, T2 * TOPK)):
                    pool.indirect_dma_start(
                        out=lists, out_offset=bass.IndirectOffsetOnAxis(ap=dest[:, n:n + 1].bitcast(U32), axis=0),
                        in_=entry[:, n, :], in_offset=None, bounds_check=NROUTED * CAP - 1,
                        oob_is_err=False).then_inc(lists_out, 16)

            def step(b, par):
                for kv in range(KV):
                    if on(b, 0):
                        low_probs(b, kv)
                    if kv == 0 and on(b, 2):
                        norm1(b + 2)
                    if kv == 3 and on(b, -1):
                        norm2(b - 1)
                    if kv in (2, 3) and on(b, 2):
                        low_q(b + 2, par, kv - 2)
                    if kv >= 3 and on(b, -3):
                        scatter(b - 3, 3 * kv - 9, 3 * kv - 6 if kv < KV - 1 else T2 * TOPK)

            loops(pool, step)
            pool.wait_ge(lists_out, 16 * T2 * TOPK * nb)
            pool.memset(slots[:], 0).then_inc(stage1, 1)
            pool.wait_ge(stage1, 4)
            pool.wait_ge(pairs_out, 16 * nb)
            pool.wait_ge(x2_out, 16 * nb)
            pool.wait_ge(xg_clear, 1)
            n0 += nb

            def gather(e, par):
                pool.wait_ge(gslots_in[par], 8 * e + 16 if par == 0 else 8 * (e + 1))
                if not is_first(e):
                    pool.wait_ge(gt_full, 8 * e)
                carry_wait(e if isinstance(e, int) and e < 2 else (CT + 1) * (e - 2) + 2)
                for c in range(CT):
                    pool.indirect_dma_start(
                        out=xg[:, c].rearrange("p a h -> p (a h)"), out_offset=None, in_=pairs,
                        in_offset=bass.IndirectOffsetOnAxis(ap=gslots[:, par, c, 0:1].bitcast(U32), axis=0),
                        bounds_check=ntok - 1, oob_is_err=False).then_inc(gathered, 16)

            def add(e, par, last):
                pool.wait_ge(slots_in[par], 8 * e + 16 if par == 0 else 8 * (e + 1))
                if not is_first(e):
                    pool.wait_ge(added, 16 * CT * e)
                for c in range(CT):
                    pool.wait_ge(y_free, 8 * e + 5 + c)
                    carry_wait((CT + 1) * e + c + 3 - (max(0, e + 3 - ne) if isinstance(e, int) else 0))
                    pool.indirect_dma_start(
                        out=o_rows, out_offset=bass.IndirectOffsetOnAxis(ap=slots[:, par, c, 0:1].bitcast(U32), axis=0),
                        in_=ys[:, c, :], in_offset=None, bounds_check=ntok - 1, oob_is_err=False,
                        compute_op=ALU.add).then_inc(added, 16)

            def step2(e, par, last):
                if not isinstance(e, int) or e + 2 < ne:
                    gather(e + 2, par)
                add(e, par, last)

            gather(0, 0)
            gather(1, 1)
            loops2(pool, step2)
            pool.wait_ge(added, 16 * CT * ne)

        @block.scalar
        def _(act):
            act.wait_ge(small_in, 64)
            act.activation(tgate[:], gates[:], ACT.Tanh).then_inc(setup_act, 1)
            act.activation(wcpair[:, 0, :], wcraw, ACT.Copy, scale=W_SCALE).then_inc(setup_act, 1)
            act.wait_ge(consts, 2)

            def hi_q(b, par, t):
                if t == 0:
                    act.wait_ge(nmr_ready, nth_norm1(b))
                    if not (isinstance(b, int) and b < 2):
                        act.wait_ge(x_full, of_p(b - 2, "Q7"))
                for c in range(2):
                    act.activation(qd[:, par, t, :, c, :], x1[:, t].rearrange("p (h d) -> p h d", d=D), ACT.Identity,
                                   scale=rstd[:, 0, t:t + 1], bias=nmr[:, 0, t:t + 1]).then_inc(qhi_ready, 1)

            def hi_k(b):
                act.wait_ge(cx_in, 16 * (b + 1))
                if not is_first(b):
                    act.wait_ge(x_full, of_p(b - 1, "K1"))
                    act.wait_ge(vd_ready, b)
                for c in (0, 2):
                    act.activation(kd[:, :, :, c * D:(c + 1) * D], cx[:], ACT.Copy, scale=C_SCALE).then_inc(khi_ready, 1)

            def hi_x(b):
                act.wait_ge(nmr_ready, nth_norm2(b))
                if not is_first(b):
                    act.wait_ge(x_full, of_r(b - 1, "X3"))
                    act.wait_ge(pairs_out, 16 * b)
                act.wait_ge(qlo_ready, 2 * min(b + 4, nb) if isinstance(b, int) else 2 * (b + 4))
                for t in range(T2):
                    for to in (xs[:, t, 0, :], xn[:, t]):
                        act.activation(to, x2[:, t], ACT.Identity, scale=rstd[:, 1, t:t + 1],
                                       bias=nmr[:, 1, t:t + 1]).then_inc(xhi_ready, 1)

            def k_stack(b, par, u):
                act.wait_ge(x_full, of_p(b, f"K{u}"))
                act.activation(ks[0:96, par, 4 * u:4 * u + 4, :].rearrange("p k s -> p (k s)"), ps_x16[0:96, :],
                               ACT.Copy).then_inc(x_free, 1)

            def q_stack(b, par, kv):
                act.wait_ge(x_full, of_p(b, f"Q{kv}"))
                act.activation(qs[0:96, par, G * kv:G * kv + G, :].rearrange("p k s -> p (k s)"), ps_x16[0:96, :],
                               ACT.Copy).then_inc(x_free, 1)

            def m_rows(b, hf):
                act.wait_ge(x_full, fill_m(b, hf))
                if not is_first(b):
                    act.wait_ge(mrow_in[hf], 32 * b)
                act.activation(mrow[:, hf, :], ps_x16[0:32, 0:S], ACT.Copy).then_inc(x_free, 1)

            def x_stack(b, u):
                act.wait_ge(x_full, of_r(b, f"X{u}"))
                act.activation(xt[:, u % 2, u // 2].rearrange("p k s -> p (k s)"), ps_x16[:, :],
                               ACT.Copy).then_inc(x_free, 1)

            def router_exp(b):
                act.wait_ge(lneg_ready, b + 1)
                for t in range(T2):
                    act.activation(lexp[:, t], lg[:, t], ACT.Exp, bias=lneg[:, t:t + 1],
                                   scale=1.0 / (XS_SCALE * W_SCALE)).then_inc(lexp_ready, 1)

            def low_done(b, kv, tt):
                if tt == 0 and kv % 2 == 0:
                    return plo_dve, 4 * b + kv // 2 + 1
                return plo_pool, 12 * b + 3 * (kv // 2) + (1 if kv % 2 == 0 else 2 + tt)

            def exps(b, kv):
                for tt in range(2):
                    u = 2 * kv + tt
                    act.wait_ge(t_full, 16 * b + u + 1)
                    if not (is_first(b) and kv < 2):
                        act.wait_ge(*(low_done(b, kv - 2, tt) if kv >= 2 else low_done(b - 1, kv + KV - 2, tt)))
                    act.activation(prob[:, u % 4], ps_t[:, tt], ACT.Exp, bias=pbias[:],
                                   scale=1.0 / (XS_SCALE * C_SCALE * float(D) ** 0.5)).then_inc(t_free, 1)

            def high_probs(b, kv):
                u = 2 * kv + 1
                act.wait_ge(t_free, 16 * b + u + 1)
                if not (is_first(b) and kv < 4):
                    act.wait_ge(v_full, 8 * b + kv - 3)
                act.activation(phi[:, u % 8], prob[:, u % 4], ACT.Copy).then_inc(phi_act, 1)

            def split_hi(e, i):
                act.wait_ge(w_in[i], 32 * (e + 1))
                if not is_first(e):
                    if i < FB:
                        act.wait_ge(gu_full, 2 * (FB * (e - 1) + i + 1))
                    else:
                        act.wait_ge(y_full, 8 * (e - 1) + 4 * (i - FB + 1))
                act.activation(wpair[:, i, 0], wraw[:, i], ACT.Copy, scale=W_SCALE).then_inc(wpair_hi, 1)

            def step(b, par):
                for kv in range(KV):
                    if kv in (0, 3) and on(b, 1):
                        k_stack(b + 1, 1 - par, kv // 3)
                    if on(b, 0):
                        exps(b, kv)
                    if on(b, 1):
                        q_stack(b + 1, 1 - par, kv)
                    if on(b, 0):
                        high_probs(b, kv)
                    if kv == 1 and on(b, 0):
                        m_rows(b, 1)
                    if kv < 3 and on(b, -2):
                        x_stack(b - 2, kv + 1)
                    if kv in (1, 2) and on(b, 2):
                        hi_q(b + 2, par, kv - 1)
                    if kv == 4 and on(b, -2):
                        router_exp(b - 2)
                    if kv == 5 and on(b, -1):
                        hi_x(b - 1)
                    if kv == 3 and on(b, 2):
                        hi_k(b + 2)
                    if kv == 5 and on(b, 1):
                        m_rows(b + 1, 0)
                    if kv == 7 and on(b, -1):
                        x_stack(b - 1, 0)
                    if kv >= 4 and at_step(b, nb + 2):
                        split_hi(0, kv - 4)

            loops(act, step)
            act.wait_ge(lexp_ready, 2 * nb)
            act.activation(tgate[:, 0:1], pbias[:], ACT.Copy).then_inc(stage1, 1)
            act.wait_ge(stage1, 4)

            def silu(e, j):
                n = FB * e + j
                act.wait_ge(gu_full, 2 * n + 1)
                if not (isinstance(n, int) and n < 2):
                    act.wait_ge(a32_ready, n - 1)
                act.activation(sg[:, j % 2], ps_gu[:, j % 2, 0], ACT.Silu, scale=1.0 / (XS_SCALE * W_SCALE)).then_inc(sg_ready, 1)

            def act_hi(e, j):
                n = FB * e + j
                act.wait_ge(a32_ready, n + 1)
                if not is_first(e) and j == 0:
                    act.wait_ge(y_full, 8 * e)
                act.activation(apair[:, 0, j], a32[:, j % 2], ACT.Copy).then_inc(ahi_ready, 1)

            def y_out(e, par, m):
                n, c = m // CT, m % CT
                act.wait_ge(y_full, 8 * e + m + 1)
                if not is_first(e) and n == 0 and c == 0:
                    act.wait_ge(added, 16 * CT * e)
                act.activation(ys[:, c, n * 512:(n + 1) * 512], ps_y[:, m % 2], ACT.Copy,
                               scale=slots[:, par, c, 1:2].bitcast(F32)).then_inc(y_free, 1)

            def step2(e, par, last):
                act.wait_ge(slots_in[par], 8 * e + 16 if par == 0 else 8 * (e + 1))
                for j in range(FB):
                    silu(e, j)
                    if j == FB - 1:
                        act_hi(e, j)
                    if AHEAD + j < CHUNKS:
                        split_hi(e, AHEAD + j)
                    elif not last:
                        split_hi(e + 1, AHEAD + j - CHUNKS)
                    if j < FB - 1:
                        act_hi(e, j)
                for m in range(8):
                    y_out(e, par, m)
                    if m in (3, 7) and not last:
                        split_hi(e + 1, 2 + m // 4)

            loops2(act, step2)

        @block.vector
        def _(dve):
            setup = Tally(dve, dve_order)

            def link(ins, tally):
                tally.add(ins)
                tally.wait()

            dve.wait_ge(setup_act, 2)
            dve.tensor_scalar(tg_at[:], tgate[:, 0:1], 1.0 / C_SCALE, None, ALU.mult).then_inc(setup_dve, 1)
            dve.tensor_scalar(tg_ff[:], tgate[:, 1:2], ROUTE_SCALE / (A_SCALE * W_SCALE), None, ALU.mult).then_inc(setup_dve, 1)
            dve.scalar_tensor_tensor(out=wcpair[:, 1, :], in0=wcraw, scalar=W_SCALE, in1=wcpair[:, 0, :],
                                     op0=ALU.mult, op1=ALU.subtract).then_inc(setup_dve, 1)
            for u in range(2):
                dve.wait_ge(wc_t, u + 1)
                dve.tensor_copy(wc[:, :, u, :], ps_x16[:, 0:KB * NALL].rearrange("p (k e) -> p k e", k=KB)).then_inc(setup_dve, 1)
            dve.wait_ge(consts, 2)
            dve.wait_ge(setup_dve, 5)

            def carry_wait(tally):
                tally.add(dve.memset(spare[:, 0:1], 0.0))

            def norm_stats(src, which, tally):
                for t in range(T2):
                    for c in range(2):
                        tally.add(dve.bn_stats(stats[:, which, t, c], src[:, t, 512 * c:512 * c + 512]))
                tally.wait()
                carry_wait(tally)
                for t in range(T2):
                    tally.add(dve.bn_aggr(mv[:, which, t], stats[:, which, t]))
                tally.wait()
                scale = XS_SCALE ** -2
                dve.tensor_scalar(veps[:, which], mv[:, which, :, 1], scale, LN_EPS * scale, ALU.mult, ALU.add).then_inc(var_ready, 1)

            def norm_shift(which, n):
                dve.wait_ge(rstd_ready, n)
                dve.scalar_tensor_tensor(out=nmr[:, which], in0=mv[:, which, :, 0], scalar=-1.0, in1=rstd[:, which],
                                         op0=ALU.mult, op1=ALU.mult).then_inc(nmr_ready, 1)

            def stats_q(b, tally):
                dve.wait_ge(x1_in, 16 * (b + 1))
                norm_stats(x1, 0, tally)

            def apply_q(b, tally):
                if not is_first(b):
                    dve.wait_ge(qlo_ready, 2 * b)
                norm_shift(0, nth_norm1(b))
                dve.wait_ge(nmr_ready, nth_norm1(b))
                for t in range(T2):
                    ins = dve.tensor_scalar(xn[:, t], x1[:, t], rstd[:, 0, t:t + 1], nmr[:, 0, t:t + 1],
                                            ALU.mult, ALU.add)
                    if t == 0:
                        tally.add(ins)
                ins.then_inc(xn_ready, 1)

            def low_k(b):
                dve.wait_ge(khi_ready, 2 * b + 2)
                dve.scalar_tensor_tensor(out=kd[:, :, :, D:2 * D].rearrange("p t k d -> p (t k) d"),
                                         in0=cx[:].rearrange("p t k d -> p (t k) d"), scalar=C_SCALE,
                                         in1=kd[:, :, :, 0:D].rearrange("p t k d -> p (t k) d"),
                                         op0=ALU.mult, op1=ALU.subtract).then_inc(kd_ready, 1)

            def keep_k(b, par):
                dve.wait_ge(kd_ready, b + 1)
                if not (isinstance(b, int) and b < 2):
                    dve.wait_ge(v_full, 8 * (b - 1))
                dve.tensor_copy(vd[:, par].rearrange("p t k d -> p (t k d)"), kd[:].rearrange("p t k d -> p (t k d)")).then_inc(vd_ready, 1)

            def maxima(b, kv, t):
                for pr in range(2):
                    n = 32 * b + 4 * kv + 2 * t + pr
                    dve.wait_ge(s_full, n + 1)
                    if kv % 4 == 0 and t == 0 and pr == 0 and not is_first(b):
                        dve.wait_ge(mpair_ready, 2 * b + kv // 4 - 1)
                    h = G * kv + 2 * pr
                    dve.tensor_reduce(mx[:, t, h:h + 2], ps_s[:, pr].rearrange("p (h s) -> p h s", h=2),
                                      AXX, ALU.max).then_inc(s_free, 1)

            def max_pairs(b, hf, tally):
                dve.wait_ge(s_free, 32 * b + 16 * (hf + 1))
                if not is_first(b):
                    dve.wait_ge(x_full, fill_m(b - 1, hf))
                src = mx[:, :, hf * 16:hf * 16 + 16]
                link(dve.tensor_scalar(mpair[:, hf, :, 0, :], src, -1.0 / M_SCALE, None, ALU.mult), tally)
                dve.scalar_tensor_tensor(out=mpair[:, hf, :, 1, :], in0=src, scalar=-1.0 / M_SCALE,
                                         in1=mpair[:, hf, :, 0, :], op0=ALU.mult, op1=ALU.subtract).then_inc(mpair_ready, 1)

            def high_probs(b, kv):
                u = 2 * kv
                dve.wait_ge(t_free, 16 * b + u + 1)
                if not (is_first(b) and kv < 4):
                    dve.wait_ge(v_full, 8 * b + kv - 3)
                dve.tensor_copy(phi[:, u % 8], prob[:, u % 4]).then_inc(phi_dve, 1)

            def low_probs(b, kv):
                u = 2 * kv
                dve.wait_ge(phi_dve, 8 * b + kv + 1)
                dve.tensor_tensor(plo[:, u % 8], prob[:, u % 4], phi[:, u % 8], ALU.subtract).then_inc(plo_dve, 1)

            def heads_out(b, kv, tally):
                dve.wait_ge(v_full, 8 * b + kv + 1)
                link(dve.reciprocal(recip[:], ps_v[:, :, :, D]), tally)
                dve.tensor_tensor(at[:, :, G * kv:G * kv + G, :], ps_v[:, :, :, 0:D],
                                  recip[:].unsqueeze(3).to_broadcast([P, T2, G, D]), ALU.mult).then_inc(v_free, 1)

            def residual(b, tally):
                dve.wait_ge(xr_in, 16 * (b + 1))
                dve.wait_ge(v_free, 8 * (b + 1))
                if not is_first(b):
                    dve.wait_ge(x2_out, 16 * b)
                    dve.wait_ge(xs_ready, b)
                dve.scalar_tensor_tensor(out=x2[:].rearrange("p t h -> p (t h)"), in0=at[:].rearrange("p t h d -> p (t h d)"),
                                         scalar=tg_at[:], in1=xr[:].rearrange("p t h -> p (t h)"),
                                         op0=ALU.mult, op1=ALU.add).then_inc(x2_ready, 1)

            def stats_x(b, tally):
                dve.wait_ge(x2_ready, b + 1)
                norm_stats(x2, 1, tally)

            def low_x(b, tally):
                for t in range(T2):
                    dve.wait_ge(xhi_ready, 4 * b + 2 * t + 2)
                    ins = dve.tensor_tensor(xs[:, t, 1], xn[:, t], xs[:, t, 0], ALU.subtract)
                    if t == 0:
                        tally.add(ins)
                ins.then_inc(xs_ready, 1)

            def bc(ap, shape):
                return ap.to_broadcast(shape)

            def router_a(b, tally):
                dve.wait_ge(x_full, of_r(b, "L"))
                dve.tensor_reduce(lg[:], ps_x[:, 0:2 * T2 * NALL].rearrange("p (t a e) -> p t e a", t=T2, a=2),
                                  AXX, ALU.add).then_inc(x_free, 1)
                dve.wait_ge(x_free, of_r(b, "L"))
                link(dve.tensor_reduce(lmax[:], lg[:], AXX, ALU.max), tally)
                dve.tensor_scalar(lneg[:], lmax[:], -1.0 / (XS_SCALE * W_SCALE), None, ALU.mult).then_inc(lneg_ready, 1)

            def router_b(b, tally):
                dve.wait_ge(lexp_ready, 2 * b + 2)
                link(dve.tensor_reduce(lsum[:], lexp[:], AXX, ALU.add), tally)
                link(dve.reciprocal(lrec[:], lsum[:]), tally)
                link(dve.tensor_tensor(score[:], lexp[:], bc(lrec[:].unsqueeze(2), [P, T2, NALL]), ALU.mult), tally)
                link(dve.tensor_tensor(biased[:], score[:], bc(bias_b[:].unsqueeze(1), [P, T2, NALL]), ALU.add), tally)
                carry_wait(tally)
                for t in range(T2):
                    tally.add(dve.max(top[:, t], biased[:, t]))
                tally.wait()
                carry_wait(tally)
                for t in range(T2):
                    tally.add(dve.max_index(topi[:, t], top[:, t], biased[:, t]))
                    tally.add(dve.match_replace(left[:, t], top[:, t], biased[:, t], -1e30))
                tally.wait()
                dve.tensor_tensor(mask[:], left[:], biased[:], ALU.not_equal).then_inc(mask_ready, 1)
                tally.add(dve.tensor_copy(topf[:], topi[:]))

            def router_w(b, tally):
                dve.wait_ge(mask_ready, b + 1)
                tally.wait()
                link(dve.tensor_tensor(wsel[:], score[:], mask[:], ALU.mult), tally)
                tally.add(dve.tensor_reduce(wsum[:, :, 0], wsel[:], AXX, ALU.add))
                tally.add(dve.tensor_reduce(wzero[:, :, 0], wsel[:, :, NROUTED:], AXX, ALU.add))
                tally.add(dve.tensor_tensor(hot[:].rearrange("p t k e -> p (t k) e"),
                                            bc(iota_e[:].unsqueeze(1), [P, T2 * TOPK, NROUTED]),
                                            bc(topf[:].rearrange("p t k -> p (t k)").unsqueeze(2), [P, T2 * TOPK, NROUTED]),
                                            ALU.is_equal))
                tally.wait()
                link(dve.tensor_scalar(wsum[:], wsum[:], ROUTE_EPS, None, ALU.add), tally)
                link(dve.reciprocal(wrec[:], wsum[:]), tally)
                link(dve.tensor_tensor(wzero[:], wzero[:], wrec[:], ALU.mult), tally)
                link(dve.tensor_scalar(wzero[:], wzero[:], ROUTE_SCALE, 1.0, ALU.mult, ALU.add), tally)
                link(dve.scalar_tensor_tensor(out=wfac[:, :, 0], in0=wzero[:, :, 0], scalar=tg_ff[:], in1=wrec[:, :, 0],
                                              op0=ALU.mult, op1=ALU.mult), tally)
                link(dve.tensor_tensor(coef[:], wsel[:, :, 0:NROUTED], bc(wfac[:], [P, T2, NROUTED]), ALU.mult), tally)

            def positions(b, tally):
                dve.wait_ge(x_full, of_r(b, "C"))
                px = ps_x[:, 0:3 * NROUTED].rearrange("p (t e) -> p t e", t=3)
                link(dve.tensor_tensor(pos[:], px[:, 0:2], bc(carry[:].unsqueeze(1), [P, T2, NROUTED]), ALU.add), tally)
                dve.tensor_tensor(carry[:], px[:, 2], carry[:], ALU.add).then_inc(x_free, 1)

            def entries(b, tally):
                tally.wait()
                link(dve.tensor_tensor(place[:], pos[:], bc(slot0[:].unsqueeze(1), [P, T2, NROUTED]), ALU.add), tally)
                link(dve.scalar_tensor_tensor(out=place[:], in0=pos[:], scalar=float(CAP), in1=place[:],
                                              op0=ALU.is_lt, op1=ALU.mult), tally)
                for w, src in ((0, place), (1, coef)):
                    for t in range(T2):
                        tally.add(dve.tensor_tensor(pick[:, w, t], hot[:, t], bc(src[:, t].unsqueeze(1), [P, TOPK, NROUTED]), ALU.mult))
                tally.wait()
                link(dve.tensor_reduce(picked[:], pick[:].rearrange("p w t k e -> p w (t k) e"), AXX, ALU.add), tally)
                if not is_first(b):
                    dve.wait_ge(lists_out, 16 * T2 * TOPK * b)
                tally.add(dve.tensor_scalar(dest[:], picked[:, 0], NO_SLOT, None, ALU.add))
                tally.add(dve.tensor_copy(entry[:, :, 1].bitcast(F32), picked[:, 1]))
                link(dve.tensor_copy(entry[:, :, 0], token[:].rearrange("p t k -> p (t k)")), tally)
                dve.tensor_scalar(token[:], token[:], float(S), None, ALU.add).then_inc(entry_ready, 1)
                dve.wait_ge(entry_ready, b + 1)

            N_A, N_PAIRS, N_OUT, N_R1, N_R2, N_R3 = 8, 1, 1, 8, 25, 10

            def own(b):
                return (N_A * on(b, 2) + N_PAIRS * (on(b, 0) + on(b, 1)) + N_OUT * (2 * on(b, -1) + 6 * on(b, 0))
                        + N_R1 * on(b, -1) + N_R2 * on(b, -2) + N_R3 * on(b, -3))

            def orders(b):
                if isinstance(b, int):
                    return sum(own(i) for i in range(-2, b))
                return orders(3) + own(3) * (b - 3)

            def split_lo(e, i):
                dve.wait_ge(wpair_hi, CHUNKS * e + i + 1)
                dve.scalar_tensor_tensor(out=wpair[:, i, 1], in0=wraw[:, i], scalar=W_SCALE, in1=wpair[:, i, 0],
                                         op0=ALU.mult, op1=ALU.subtract).then_inc(wpair_lo, 1)

            def step(b, par):
                tally = Tally(dve, dve_order, orders(b))

                def scored(kv, t):
                    if kv == 0 and on(b, 0):
                        maxima(b, KV - 1, t)
                    if kv > 0 and on(b, 1):
                        maxima(b + 1, kv - 1, t)

                for kv in range(KV):
                    scored(kv, 0)
                    if on(b, 0):
                        high_probs(b, kv)
                        if kv % 2 == 0:
                            low_probs(b, kv)
                    if kv == 0 and on(b, 2):
                        stats_q(b + 2, tally)
                    if kv == 1 and on(b, 2):
                        apply_q(b + 2, tally)
                    if kv == 3 and on(b, -3):
                        entries(b - 3, tally)
                    if kv == 2 and on(b, -1):
                        stats_x(b - 1, tally)
                    if kv == 4 and on(b, -1):
                        norm_shift(1, nth_norm2(b - 1))
                    if kv == 6 and on(b, -1):
                        low_x(b - 1, tally)
                    scored(kv, 1)
                    if kv < 2 and on(b, -1):
                        heads_out(b - 1, kv + KV - 2, tally)
                    if kv >= 2 and on(b, 0):
                        heads_out(b, kv - 2, tally)
                    if kv == 0 and on(b, 0):
                        max_pairs(b, 1, tally)
                    if kv == 1 and on(b, -1):
                        residual(b - 1, tally)
                    if kv == 2 and on(b, 1):
                        keep_k(b + 1, 1 - par)
                    if kv == 3 and on(b, -2):
                        router_a(b - 2, tally)
                    if kv == 4 and on(b, 1):
                        max_pairs(b + 1, 0, tally)
                    if kv == 4 and on(b, 2):
                        low_k(b + 2)
                    if kv == 5 and on(b, -2):
                        router_b(b - 2, tally)
                    if kv == 6 and on(b, -2):
                        positions(b - 2, tally)
                        router_w(b - 2, tally)
                    if kv > 4 and at_step(b, nb + 2):
                        split_lo(0, kv - 5)
                    if kv == 4 and at_step(b, nb + 2):
                        dve.memset(xg[:], 0.0).then_inc(xg_clear, 1)
                tally.close(own(b))

            loops(dve, step)
            dve.wait_ge(x_free, of_r(nb - 1, "C"))
            dve.tensor_copy(filled[:], carry[0:1, :]).then_inc(stage1, 1)
            dve.wait_ge(stage1, 4)

            def take_t(e, par, u):
                c, part = u // 2, u % 2
                dve.wait_ge(gt_full, 8 * e + u + 1)
                dve.tensor_copy(xgt[:, par, part, :, c * P:(c + 1) * P],
                                ps_g16[u % 2].rearrange("p (k t) -> p k t", k=KB)).then_inc(gt_free, 1)

            def gate_up(e, j):
                n = FB * e + j
                dve.wait_ge(gu_full, 2 * n + 2)
                dve.wait_ge(sg_ready, n + 1)
                if not (isinstance(n, int) and n < 2):
                    dve.wait_ge(alo_ready, n - 1)
                dve.scalar_tensor_tensor(out=a32[:, j % 2], in0=ps_gu[:, j % 2, 1],
                                         scalar=A_SCALE / (XS_SCALE * W_SCALE), in1=sg[:, j % 2],
                                         op0=ALU.mult, op1=ALU.mult).then_inc(a32_ready, 1)

            def act_lo(e, j):
                n = FB * e + j
                dve.wait_ge(ahi_ready, n + 1)
                dve.tensor_tensor(apair[:, 1, j], a32[:, j % 2], apair[:, 0, j], ALU.subtract).then_inc(alo_ready, 1)

            def step2(e, par, last):
                for j in range(FB):
                    if not last:
                        for u in ROWS_AFTER[j][:2]:
                            take_t(e + 1, 1 - par, u)
                    gate_up(e, j)
                    if j < FB - 1 and AHEAD + j - 1 < CHUNKS:
                        split_lo(e, AHEAD + j - 1)
                    act_lo(e, j)
                    if not last:
                        for u in ROWS_AFTER[j][2:]:
                            take_t(e + 1, 1 - par, u)
                if not last:
                    for i in range(AHEAD - 1):
                        split_lo(e + 1, i)

            for u in range(8):
                take_t(0, 0, u)
            loops2(dve, step2)

        @block.tensor
        def _(pe):
            pe.wait_ge(consts, 2)
            pe.wait_ge(setup_act, 2)
            pe.wait_ge(setup_dve, 3)
            for u in range(2):
                if u:
                    pe.wait_ge(setup_dve, 4)
                for k in range(KB):
                    mm = pe.transpose(ps_x16[:, k * NALL:(k + 1) * NALL], wcpair[:, u, k * P:(k + 1) * P], ident[0:NALL, 0:NALL])
                mm.then_inc(wc_t, 1)
            pe.wait_ge(setup_dve, 5)

            def take_bank(n):
                if not (isinstance(n, int) and n == 1):
                    pe.wait_ge(x_free, n - 1)

            def k_transpose(b, u):
                pe.wait_ge(kd_ready, b + 1)
                take_bank(of_p(b, f"K{u}"))
                for k in range(4):
                    for t in range(T2):
                        mm = pe.transpose(ps_x16[0:96, k * S + t * P:k * S + (t + 1) * P], kd[:, t, 4 * u + k, 0:96], ident[:])
                mm.then_inc(x_full, 1)

            def q_transpose(b, par, kv):
                if kv == 0:
                    pe.wait_ge(qlo_ready, 2 * (b + 1))
                take_bank(of_p(b, f"Q{kv}"))
                for g in range(G):
                    for t in range(T2):
                        mm = pe.transpose(ps_x16[0:96, g * S + t * P:g * S + (t + 1) * P],
                                          qd[:, par, t, G * kv + g].rearrange("p c d -> p (c d)"), ident[:])
                mm.then_inc(x_full, 1)

            def m_transpose(b, hf):
                pe.wait_ge(mpair_ready, 2 * b + hf + 1)
                take_bank(fill_m(b, hf))
                for t in range(T2):
                    mm = pe.transpose(ps_x16[0:32, t * P:(t + 1) * P], mpair[:, hf, t].rearrange("p a h -> p (a h)"), ident[:])
                mm.then_inc(x_full, 1)

            def scores(b, par, kv, t):
                if t == 0:
                    pe.wait_ge(x_free, of_p(b, f"Q{kv}"))
                for pr in range(2):
                    n = 32 * b + 4 * kv + 2 * t + pr
                    if not (isinstance(n, int) and n < 2):
                        pe.wait_ge(s_free, n - 1)
                    for i in range(2):
                        h = G * kv + 2 * pr + i
                        mm = pe.matmul(ps_s[:, pr, i * S:(i + 1) * S], qs[0:96, par, h, t * P:(t + 1) * P],
                                       ks[0:96, par, kv, :], start=True, stop=True)
                    mm.then_inc(s_full, 1)

            def scores_t(b, par, kv):
                if kv % 4 == 0:
                    pe.wait_ge(mrow_in[kv // 4], 32 * (b + 1))
                for tt in range(2):
                    n = 16 * b + 2 * kv + tt
                    if not (isinstance(n, int) and n < 2):
                        pe.wait_ge(t_free, n - 1)
                    for pr in range(2):
                        h = G * kv + 2 * pr
                        mm = pe.matmul(ps_t[:, tt, 512 * pr:512 * pr + 512], ks[0:98, par, kv, tt * P:(tt + 1) * P],
                                       qs[0:98, par, h:h + 2, :], start=True, stop=True)
                    mm.then_inc(t_full, 1)

            def values(b, par, kv):
                if kv % 2 == 0:
                    pe.wait_ge(plo_dve, 4 * b + kv // 2 + 1)
                pe.wait_ge(plo_pool, 12 * b + 3 * (kv // 2) + (1 if kv % 2 == 0 else 3))
                if kv == 0:
                    pe.wait_ge(vd_ready, b + 1)
                n = 8 * b + kv
                if not (isinstance(n, int) and n == 0):
                    pe.wait_ge(v_free, n)
                for t in range(T2):
                    for g in range(G):
                        c0 = g * S + t * P
                        for tt in range(2):
                            r = (2 * kv + tt) % 8
                            pe.matmul(ps_v[:, t, g, :], phi[:, r, c0:c0 + P], vd[:, par, tt, kv, 64:97],
                                      start=(tt == 0), stop=False)
                            pe.matmul(ps_v[:, t, g, 0:D], phi[:, r, c0:c0 + P], vd[:, par, tt, kv, D:2 * D],
                                      start=False, stop=False)
                            mm = pe.matmul(ps_v[:, t, g, :], plo[:, r, c0:c0 + P], vd[:, par, tt, kv, 64:97],
                                           start=False, stop=(tt == 1))
                mm.then_inc(v_full, 1)

            def x_transpose(b, u):
                if u == 0:
                    pe.wait_ge(xs_ready, b + 1)
                take_bank(of_r(b, f"X{u}"))
                for k in range(KB):
                    mm = pe.transpose(ps_x16[:, k * P:(k + 1) * P], xs[:, u // 2, u % 2, k * P:(k + 1) * P], ident[:])
                mm.then_inc(x_full, 1)

            def logits(b):
                pe.wait_ge(x_free, of_r(b, "X3"))
                take_bank(of_r(b, "L"))
                for t in range(T2):
                    for part in range(2):
                        for k in range(KB):
                            mm = pe.matmul(ps_x[:, t * 2 * NALL:(t + 1) * 2 * NALL], xt[:, part, t, k, :],
                                           wc[:, k].rearrange("p a e -> p (a e)"), start=(part == 0 and k == 0),
                                           stop=(part == 1 and k == KB - 1))
                mm.then_inc(x_full, 1)

            def counts(b):
                pe.wait_ge(mask_ready, b + 1)
                take_bank(of_r(b, "C"))
                m0, m1 = mask[:, 0, 0:NROUTED], mask[:, 1, 0:NROUTED]
                n = NROUTED
                pe.matmul(ps_x[:, 0:n], tri[:], m0, start=True, stop=True)
                pe.matmul(ps_x[:, n:2 * n], ones[:], m0, start=True, stop=False)
                pe.matmul(ps_x[:, n:2 * n], tri[:], m1, start=False, stop=True)
                pe.matmul(ps_x[:, 2 * n:3 * n], ones[:], m0, start=True, stop=False)
                pe.matmul(ps_x[:, 2 * n:3 * n], ones[:], m1, start=False, stop=True).then_inc(x_full, 1)

            def step(b, par):
                def scored(kv, t):
                    if kv == 0 and on(b, 0):
                        scores(b, par, KV - 1, t)
                    if kv > 0 and on(b, 1):
                        scores(b + 1, 1 - par, kv - 1, t)

                for kv in range(KV):
                    if kv in (0, 3) and on(b, 1):
                        k_transpose(b + 1, kv // 3)
                    if on(b, 0):
                        scores_t(b, par, kv)
                    scored(kv, 0)
                    if on(b, 1):
                        q_transpose(b + 1, 1 - par, kv)
                    if kv == 0 and on(b, -2):
                        x_transpose(b - 2, 1)
                    if kv < 2 and on(b, -1):
                        values(b - 1, 1 - par, kv + KV - 2)
                    if kv >= 2 and on(b, 0):
                        values(b, par, kv - 2)
                    if kv == 1 and on(b, 0):
                        m_transpose(b, 1)
                    if kv in (1, 2) and on(b, -2):
                        x_transpose(b - 2, kv + 1)
                    if kv == 3 and on(b, -2):
                        logits(b - 2)
                    if kv == 5 and on(b, 1):
                        m_transpose(b + 1, 0)
                    if kv == 6 and on(b, -2):
                        counts(b - 2)
                    if kv == 7 and on(b, -1):
                        x_transpose(b - 1, 0)
                    scored(kv, 1)

            loops(pe, step)
            pe.wait_ge(x_free, of_r(nb - 1, "C"))
            pe.transpose(ps_x16[0:32, 0:P], ident[:, 0:32], ident[:]).then_inc(stage1, 1)
            pe.wait_ge(stage1, 4)

            def t_rows(e, us):
                for u in us:
                    c, part = u // 2, u % 2
                    if u == 0:
                        pe.wait_ge(gathered, 16 * CT * (e + 1))
                    n = 8 * e + u
                    if not (isinstance(n, int) and n < 2):
                        pe.wait_ge(gt_free, n - 1)
                    for k in range(KB):
                        mm = pe.transpose(ps_g16[u % 2][:, k * P:(k + 1) * P], xg[:, c, part, k * P:(k + 1) * P], ident[:])
                    mm.then_inc(gt_full, 1)

            TERMS = ((0, 0), (0, 1), (1, 0))

            def up(e, par, j, nt):
                n = FB * e + j
                pe.wait_ge(wpair_lo, CHUNKS * e + j + 1)
                if j == 0:
                    pe.wait_ge(gt_free, 8 * e + 8)
                if not (isinstance(n, int) and n < 2):
                    pe.wait_ge(a32_ready, n - 1)
                w = wpair[:, j].rearrange("p a (k h f) -> p a k h f", k=KB, h=2)
                for h in range(2):
                    for k in range(KB):
                        for a, c in TERMS:
                            mm = pe.matmul(ps_gu[:, j % 2, h, 0:nt * P], w[:, a, k, h, :], xgt[:, par, c, k, 0:nt * P],
                                           start=(k == 0 and (a, c) == (0, 0)), stop=(k == KB - 1 and a == 1))
                    mm.then_inc(gu_full, 1)

            def down(e, n2, nt):
                i = FB + n2
                pe.wait_ge(wpair_lo, CHUNKS * e + i + 1)
                w = wpair[:, i].rearrange("p a (k h) -> p a k h", k=FB)
                for c in range(nt):
                    m = CT * n2 + c
                    n = 8 * e + m
                    if not (isinstance(n, int) and n < 2):
                        pe.wait_ge(y_free, n - 1)
                    for k in range(FB):
                        if m == 0 and k in (0, FB - 1):
                            pe.wait_ge(alo_ready, FB * e + (FB if k else FB - 1))
                        for a, o in ((0, 0), (1, 0), (0, 1)):
                            mm = pe.matmul(ps_y[:, m % 2], apair[:, o, k, c * P:(c + 1) * P], w[:, a, k, :],
                                           start=(k == 0 and (a, o) == (0, 0)), stop=(k == FB - 1 and o == 1))
                    mm.then_inc(y_full, 1 if c < nt - 1 else 1 + CT - nt)

            def products(e, par, last, nt):
                for j in range(FB):
                    up(e, par, j, nt)
                    if not last:
                        t_rows(e + 1, ROWS_AFTER[j])
                for n2 in range(2):
                    down(e, n2, nt)

            def step2(e, par, last):
                if is_first(e):
                    products(e, par, last, CT)
                    return
                n = pe.value_load(filled[0:1, bass.ds(e, 1)], min_val=0, max_val=ntok)
                with pe.If(n < 2 * P + 1):
                    with pe.If(n < P + 1):
                        products(e, par, last, 1)
                    with pe.Else():
                        products(e, par, last, 2)
                with pe.Else():
                    with pe.If(n < 3 * P + 1):
                        products(e, par, last, 3)
                    with pe.Else():
                        products(e, par, last, 4)

            t_rows(0, range(8))
            loops2(pe, step2)


_INS = ['x', 'ctx_512', 'g_xattn', 'g_ffn', 'L0_ffn_w_cls', 'L0_ffn_bias', 'L0_ffn_w_gate_up', 'L0_ffn_w_down']
_OUTS = [((16, 256, 1024), 'float32')]


def kernel(**inputs):
    import numpy as _np
    import concourse.bacc as _bacc
    from concourse import mybir as _mybir
    from concourse.bass_utils import run_bass_kernel_spmd as _run

    nc = _bacc.Bacc("TRN2", target_bir_lowering=False, num_devices=1)
    arrays, args = {}, []
    for name in _INS:
        a = _np.ascontiguousarray(inputs[name])
        arrays[f"in_{name}_dram"] = a
        args.append(nc.dram_tensor(f"in_{name}_dram", a.shape, _mybir.dt.from_np(a.dtype), kind="ExternalInput").ap())
    for i, (shape, dtype) in enumerate(_OUTS):
        dt = _mybir.dt.from_np(_np.dtype(dtype))
        args.append(nc.dram_tensor(f"out_{i}_dram", shape, dt, kind="ExternalOutput").ap())
    gated_block_kernel(nc, *args)
    r = _run(nc, [arrays], core_ids=[0])
    return r.results[0]["out_0_dram"]
```
